# Optimizing a Trainium2 kernel written in Bass

```python
import numpy as np
import jax
import jax.numpy as jnp

def _softmax(x, axis=-1):
    return jax.nn.softmax(x, axis=axis)

def _gelu(x):
    return jax.nn.gelu(x, approximate=True)

def _silu(x):
    return jax.nn.silu(x)

def _sigmoid(x):
    return jax.nn.sigmoid(x)

def _layernorm(x, axis=-1, eps=1e-05):
    m = jnp.mean(x, axis=axis, keepdims=True)
    v = jnp.var(x, axis=axis, keepdims=True)
    return (x - m) / jnp.sqrt(v + eps)

def _scatter_add(tgt, idx, src, axis=0):
    return tgt.at[idx].add(src)

def _segment_sum(src, seg, n):
    return jax.ops.segment_sum(src, seg, n)
kernel_name = 'mk_gnn_resnorm_d4_gnn_r32_61b624'

def setup_inputs(seed: int=0):
    np.random.seed(seed)
    _w = jnp.asarray

    def _rec_inputs():
        import jax
        import jax.numpy as jnp
        _gk = jax.random.key(seed)
        x = -0.000202 + 1 * jax.random.normal(jax.random.fold_in(_gk, 1), (3125, 64), jnp.float32)
        src = jax.random.randint(jax.random.fold_in(_gk, 2), (100000,), 0, 3125, jnp.int32)
        dst = jax.random.randint(jax.random.fold_in(_gk, 3), (100000,), 0, 3125, jnp.int32)
        _o = jnp.argsort(dst, stable=True)
        src = src[_o]
        dst = dst[_o]
        edge_attr_64 = 0.000189758 + 1.00013 * jax.random.normal(jax.random.fold_in(_gk, 13), (100000, 64), jnp.float32)
        edge_type_8 = jax.random.randint(jax.random.fold_in(_gk, 15), (100000,), 0, 8, jnp.int32)
        return (x, src, dst, edge_attr_64, edge_type_8)
    x, src, dst, edge_attr_64, edge_type_8 = _rec_inputs()

    def _L0_gnn_setup():
        import jax, jax.numpy as jnp
        import numpy as np
        NEG_SLOPE = 0.2

        def _gat_relation(x, src, dst, mask, N, Wr, a_src, a_dst, br):
            h = x @ Wr
            s = h @ a_src
            d = h @ a_dst
            e = jax.nn.leaky_relu(s[src] + d[dst], negative_slope=NEG_SLOPE)
            e = jnp.where(mask, e, -jnp.inf)
            m = jax.ops.segment_max(e, dst, num_segments=N)
            w = jnp.where(mask, jnp.exp(e - m[dst]), 0.0)
            denom = jax.ops.segment_sum(w, dst, num_segments=N)
            alpha = w / denom[dst]
            msg = alpha[:, None] * h[src]
            return jax.ops.segment_sum(msg, dst, num_segments=N) + br
        key = jax.random.key(seed)
        ks = jax.random.split(key, 9)
        N, E, D, F, R = (3125, 50000, 64, 64, 8)
        x = jax.random.normal(ks[0], (N, D), dtype=jnp.float32)
        edge_index = jax.random.randint(ks[1], (2, E), 0, N, dtype=jnp.int32)
        edge_type = jax.random.randint(ks[2], (E,), 0, R, dtype=jnp.int32)
        W_self = jax.random.normal(ks[3], (D, F), dtype=jnp.float32) * 0.1
        b_self = jax.random.normal(ks[4], (F,), dtype=jnp.float32) * 0.1
        W = jax.random.normal(ks[5], (R, D, F), dtype=jnp.float32) * 0.1
        att_src = jax.random.normal(ks[6], (R, F), dtype=jnp.float32) * 0.1
        att_dst = jax.random.normal(ks[7], (R, F), dtype=jnp.float32) * 0.1
        bias = jax.random.normal(ks[8], (R, F), dtype=jnp.float32) * 0.1
        return {'x': x, 'edge_index': edge_index, 'edge_type': edge_type, 'W_self': W_self, 'b_self': b_self, 'W': W, 'att_src': att_src, 'att_dst': att_dst, 'bias': bias}
    _L0_gnn_all = _L0_gnn_setup()
    _L0_gnn_in = {k: v for k, v in _L0_gnn_all.items() if k in ('W_self', 'b_self', 'W', 'att_src', 'att_dst', 'bias')}
    del _L0_gnn_all

    def _L1_gnn_setup():
        import jax, jax.numpy as jnp
        import numpy as np
        N_NODES = 3125
        N_EDGES = 50000
        D_IN = 64
        D_OUT = 64
        key = jax.random.key(seed)
        k1, k2, k3, k4, k5 = jax.random.split(key, 5)
        feat = jax.random.normal(k1, (N_NODES, D_IN), dtype=jnp.float32)
        weight1 = jax.random.normal(k2, (D_IN, D_OUT), dtype=jnp.float32) * (1.0 / np.sqrt(D_IN))
        weight2 = jax.random.normal(k3, (D_IN, D_OUT), dtype=jnp.float32) * (1.0 / np.sqrt(D_IN))
        src = jax.random.randint(k4, (N_EDGES,), 0, N_NODES, dtype=jnp.int32)
        dst = jax.random.randint(k5, (N_EDGES,), 0, N_NODES, dtype=jnp.int32)
        return {'feat': feat, 'weight1': weight1, 'weight2': weight2, 'src': src, 'dst': dst}
    _L1_gnn_all = _L1_gnn_setup()
    _L1_gnn_in = {k: v for k, v in _L1_gnn_all.items() if k in ('weight1', 'weight2')}
    del _L1_gnn_all

    def _L2_gnn_setup():
        import jax, jax.numpy as jnp
        import numpy as np
        N_NODES = 50000
        N_EDGES = 25000
        D = 64
        N_LAYERS = 3
        key = jax.random.key(seed)
        ks = jax.random.split(key, 5)
        x = jax.random.normal(ks[0], (N_NODES, D), dtype=jnp.float32)
        edge_index = jax.random.randint(ks[1], (2, N_EDGES), 0, N_NODES, dtype=jnp.int64)
        scale = 1.0 / np.sqrt(D)
        W_msg = jax.random.normal(ks[2], (N_LAYERS, D, D), dtype=jnp.float32) * scale
        W_self = jax.random.normal(ks[3], (N_LAYERS, D, D), dtype=jnp.float32) * scale
        b = jax.random.normal(ks[4], (N_LAYERS, D), dtype=jnp.float32) * 0.01
        return {'x': x, 'edge_index': edge_index, 'W_msg': W_msg, 'W_self': W_self, 'b': b}
    _L2_gnn_all = _L2_gnn_setup()
    _L2_gnn_in = {k: v for k, v in _L2_gnn_all.items() if k in ('W_msg', 'W_self', 'b')}
    del _L2_gnn_all

    def _L3_gnn_setup():
        import jax, jax.numpy as jnp
        import numpy as np
        N_NODES = 50000
        N_EDGES = 25000
        D_NODE = 64
        D_EDGE = 64
        D_H = 128
        D_U = 32
        D_OUT = 64
        N_GRAPHS = 16
        key = jax.random.key(seed)
        ks = jax.random.split(key, 16)
        x = jax.random.normal(ks[0], (N_NODES, D_NODE), dtype=jnp.float32)
        edge_index = jax.random.randint(ks[1], (2, N_EDGES), 0, N_NODES, dtype=jnp.int64)
        edge_attr = jax.random.normal(ks[2], (N_EDGES, D_EDGE), dtype=jnp.float32)
        u = jax.random.normal(ks[3], (N_GRAPHS, D_U), dtype=jnp.float32)
        batch = jnp.sort(jax.random.randint(ks[4], (N_NODES,), 0, N_GRAPHS, dtype=jnp.int64))
        s = 0.05
        W1 = jax.random.normal(ks[5], (D_H, D_NODE + D_EDGE), dtype=jnp.float32) * s
        b1 = jax.random.normal(ks[6], (D_H,), dtype=jnp.float32) * s
        W2 = jax.random.normal(ks[7], (D_H, D_H), dtype=jnp.float32) * s
        b2 = jax.random.normal(ks[8], (D_H,), dtype=jnp.float32) * s
        Wa = jax.random.normal(ks[9], (D_H, D_NODE + D_H + D_U), dtype=jnp.float32) * s
        ba = jax.random.normal(ks[10], (D_H,), dtype=jnp.float32) * s
        Wb = jax.random.normal(ks[11], (D_OUT, D_H), dtype=jnp.float32) * s
        bb = jax.random.normal(ks[12], (D_OUT,), dtype=jnp.float32) * s
        return {'x': x, 'edge_index': edge_index, 'edge_attr': edge_attr, 'u': u, 'batch': batch, 'W1': W1, 'b1': b1, 'W2': W2, 'b2': b2, 'Wa': Wa, 'ba': ba, 'Wb': Wb, 'bb': bb}
    _L3_gnn_all = _L3_gnn_setup()
    _L3_gnn_in = {k: v for k, v in _L3_gnn_all.items() if k in ('u', 'W1', 'b1', 'W2', 'b2', 'Wa', 'ba', 'Wb', 'bb')}
    del _L3_gnn_all
    return {'x': x, 'src': src, 'dst': dst, 'edge_attr_64': edge_attr_64, 'edge_type_8': edge_type_8, 'L0_gnn_W_self': _L0_gnn_in['W_self'], 'L0_gnn_b_self': _L0_gnn_in['b_self'], 'L0_gnn_W': _L0_gnn_in['W'], 'L0_gnn_att_src': _L0_gnn_in['att_src'], 'L0_gnn_att_dst': _L0_gnn_in['att_dst'], 'L0_gnn_bias': _L0_gnn_in['bias'], 'L1_gnn_weight1': _L1_gnn_in['weight1'], 'L1_gnn_weight2': _L1_gnn_in['weight2'], 'L2_gnn_W_msg': _L2_gnn_in['W_msg'], 'L2_gnn_W_self': _L2_gnn_in['W_self'], 'L2_gnn_b': _L2_gnn_in['b'], 'L3_gnn_u': _L3_gnn_in['u'], 'L3_gnn_W1': _L3_gnn_in['W1'], 'L3_gnn_b1': _L3_gnn_in['b1'], 'L3_gnn_W2': _L3_gnn_in['W2'], 'L3_gnn_b2': _L3_gnn_in['b2'], 'L3_gnn_Wa': _L3_gnn_in['Wa'], 'L3_gnn_ba': _L3_gnn_in['ba'], 'L3_gnn_Wb': _L3_gnn_in['Wb'], 'L3_gnn_bb': _L3_gnn_in['bb']}

def reference(x, src, dst, edge_attr_64, edge_type_8, L0_gnn_W_self, L0_gnn_b_self, L0_gnn_W, L0_gnn_att_src, L0_gnn_att_dst, L0_gnn_bias, L1_gnn_weight1, L1_gnn_weight2, L2_gnn_W_msg, L2_gnn_W_self, L2_gnn_b, L3_gnn_u, L3_gnn_W1, L3_gnn_b1, L3_gnn_W2, L3_gnn_b2, L3_gnn_Wa, L3_gnn_ba, L3_gnn_Wb, L3_gnn_bb):
    import jax
    import jax.numpy as jnp

    def _L0_gnn_ref(x, edge_index, edge_type, W_self, b_self, W, att_src, att_dst, bias):
        import jax, jax.numpy as jnp
        import numpy as np
        NEG_SLOPE = 0.2

        def _gat_relation(x, src, dst, mask, N, Wr, a_src, a_dst, br):
            h = x @ Wr
            s = h @ a_src
            d = h @ a_dst
            e = jax.nn.leaky_relu(s[src] + d[dst], negative_slope=NEG_SLOPE)
            e = jnp.where(mask, e, -jnp.inf)
            m = jax.ops.segment_max(e, dst, num_segments=N)
            w = jnp.where(mask, jnp.exp(e - m[dst]), 0.0)
            denom = jax.ops.segment_sum(w, dst, num_segments=N)
            alpha = w / denom[dst]
            msg = alpha[:, None] * h[src]
            return jax.ops.segment_sum(msg, dst, num_segments=N) + br
        N = x.shape[0]
        R = W.shape[0]
        loops = jnp.arange(N, dtype=edge_index.dtype)
        src = jnp.concatenate([edge_index[0], loops])
        dst = jnp.concatenate([edge_index[1], loops])
        ones_loops = jnp.ones((N,), dtype=bool)
        out = x @ W_self + b_self
        for r in range(R):
            mask = jnp.concatenate([edge_type == r, ones_loops])
            out = out + _gat_relation(x, src, dst, mask, N, W[r], att_src[r], att_dst[r], bias[r])
        return out

    def _L1_gnn_ref(feat, weight1, weight2, src, dst):
        import jax, jax.numpy as jnp
        import numpy as np
        N_NODES = 3125
        N_EDGES = 50000
        D_IN = 64
        D_OUT = 64
        N = feat.shape[0]
        ones_e = jnp.ones(src.shape[0], dtype=feat.dtype)
        out_deg = jnp.clip(jax.ops.segment_sum(ones_e, src, num_segments=N), 1.0)
        feat_n = feat * jax.lax.rsqrt(out_deg)[:, None]
        h_src = feat_n[src]
        copy_sum = jax.ops.segment_sum(h_src, dst, num_segments=N)
        inner_sum = jax.ops.segment_sum(h_src * feat_n[dst], dst, num_segments=N)
        rst = copy_sum @ weight1 + inner_sum @ weight2
        in_deg = jnp.clip(jax.ops.segment_sum(ones_e, dst, num_segments=N), 1.0)
        rst = rst * jax.lax.rsqrt(in_deg)[:, None]
        return rst

    def _L2_gnn_ref(x, edge_index, W_msg, W_self, b):
        import jax, jax.numpy as jnp
        import numpy as np
        N_NODES = 50000
        N_EDGES = 25000
        D = 64
        N_LAYERS = 3
        'Stacked sheaf conv layers: per-edge gather -> linear restriction ->\n            scatter-sum aggregation to destination nodes + self-loop linear + bias,\n            with ReLU between layers (none after the final layer).'
        n = x.shape[0]
        src, dst = (edge_index[0], edge_index[1])
        n_layers = W_msg.shape[0]
        for i in range(n_layers):
            msg = x[src] @ W_msg[i]
            agg = jax.ops.segment_sum(msg, dst, num_segments=n)
            x = x @ W_self[i] + agg + b[i]
            if i < n_layers - 1:
                x = jax.nn.relu(x)
        return x

    def _L3_gnn_ref(x, edge_index, edge_attr, u, batch, W1, b1, W2, b2, Wa, ba, Wb, bb):
        import jax, jax.numpy as jnp
        import numpy as np
        N_NODES = 50000
        N_EDGES = 25000
        D_NODE = 64
        D_EDGE = 64
        D_H = 128
        D_U = 32
        D_OUT = 64
        N_GRAPHS = 16
        row, col = (edge_index[0], edge_index[1])
        h = jnp.concatenate([x[col], edge_attr], axis=1)
        h = jax.nn.relu(h @ W1.T + b1)
        h = jax.nn.relu(h @ W2.T + b2)
        n = x.shape[0]
        summed = jax.ops.segment_sum(h, row, num_segments=n)
        cnt = jax.ops.segment_sum(jnp.ones((h.shape[0],), dtype=h.dtype), row, num_segments=n)
        agg = summed / jnp.maximum(cnt, 1.0)[:, None]
        z = jnp.concatenate([x, agg, u[batch]], axis=1)
        z = jax.nn.relu(z @ Wa.T + ba)
        return z @ Wb.T + bb
    edge_index = jnp.stack([src, dst])
    batch0 = jnp.zeros((3125,), jnp.int32)
    x = _layernorm(x + _L0_gnn_ref(x, edge_index, edge_type_8, L0_gnn_W_self, L0_gnn_b_self, L0_gnn_W, L0_gnn_att_src, L0_gnn_att_dst, L0_gnn_bias), axis=-1)
    x = _layernorm(x + _L1_gnn_ref(x, L1_gnn_weight1, L1_gnn_weight2, src, dst), axis=-1)
    x = _layernorm(x + _L2_gnn_ref(x, edge_index, L2_gnn_W_msg, L2_gnn_W_self, L2_gnn_b), axis=-1)
    x = _layernorm(x + _L3_gnn_ref(x, edge_index, edge_attr_64, L3_gnn_u, batch0, L3_gnn_W1, L3_gnn_b1, L3_gnn_W2, L3_gnn_b2, L3_gnn_Wa, L3_gnn_ba, L3_gnn_Wb, L3_gnn_bb), axis=-1)
    return x

_drawn_inputs = setup_inputs


def setup_inputs(seed=0):
    import zlib

    import numpy as np

    out = dict(_drawn_inputs(seed))
    spreads = {}
    factors = {'edge_attr_64': 8.0,
     'L0_gnn_att_dst': 19.931,
     'L2_gnn_b': 45.351,
     'L3_gnn_b1': 8.0,
     'L3_gnn_W2': 3.07,
     'L3_gnn_b2': 8.0,
     'L3_gnn_ba': 2.878}
    for name, (base, spread) in spreads.items():
        noise = np.random.default_rng([zlib.crc32(name.encode()), seed]).standard_normal(out[name].shape)
        drawn = base * np.exp(spread * noise) if base else spread * noise
        out[name] = jnp.asarray(drawn.astype(out[name].dtype))
    for name, factor in factors.items():
        out[name] = (out[name] * factor).astype(out[name].dtype)
    return out
```

```python
from contextlib import ExitStack

import concourse.bass as bass
from concourse import mybir
from concourse.alu_op_type import AluOpType as ALU

ACT = mybir.ActivationFunctionType
AX = mybir.AxisListType.X
F32 = mybir.dt.float32
BF16 = mybir.dt.bfloat16
I32 = mybir.dt.int32
U32 = mybir.dt.uint32

P = 128
N = 3125
E = 100000
D = 64
R = 8
H = 128
DU = 32
NT = -(-N // P)
NP = NT * P
PAD_NODE = -(-N // 16) * 16
EC = -(-E // P)
EP = EC * P
GN = P // R
NG = PAD_NODE // GN + 1
GW = 208
B = 8
NB0 = -(-((E + (NG - 1) * (P - 1)) // P + -(-(EP - E) // P)) // (2 * B)) * 2
NB3 = -(-(EC + NT + 1) // (2 * B)) * 2
NV = P * B
AC = -(-EC // (NB0 // 2))
AE = AC * (NB0 // 2)
CR = (EP + P) // (NB0 // 2)
TRASH = NP * NP
RW = 4 + D
TW = D + 2
SPARE = NP
NACC = 4
BIG = float(2.0 ** 100)
SLOPE = 0.2
EPS = 1e-5
ZERO_FIRST, ZERO_NEXT = 11, 16
CW = 512
DC = -(-NP // CW)

assert NB0 * B <= NV and NB3 * B <= NV and NG < GW
assert AC <= 14

class Steps:

    def __init__(self, eng, sem):
        self.eng, self.sem, self.n = eng, sem, 0

    def __call__(self, ins):
        self.n += 1
        ins.then_inc(self.sem, 1)
        self.eng.wait_ge(self.sem, self.n)
        return self.n

class Stage(ExitStack):

    def __init__(self, nc):
        super().__init__()
        self.nc, self.sems = nc, []
        self.callback(self.give_back)

    def give_back(self):
        self.nc.clear_and_free_semaphores(self.sems)
        self.nc.all_engine_barrier()

    def semaphore(self, name):
        self.sems.append(self.nc.alloc_semaphore(name=name))
        return self.sems[-1]

def constants(nc, k):
    with Stage(nc) as c:
        const_step = c.semaphore("const_step")
        block = c.enter_context(nc.Block())

        @block.gpsimd
        def _(pool):
            step = Steps(pool, const_step)
            nc.gpsimd.iota(k.iota_row[:], [[1, P]], base=0, channel_multiplier=0,
                           allow_small_or_imprecise_dtypes=True)
            nc.gpsimd.iota(k.visit_col[:], [[1, B]], base=0, channel_multiplier=B,
                           allow_small_or_imprecise_dtypes=True)
            nc.gpsimd.iota(k.trash_col[:], [[P, 8]], base=TRASH, channel_multiplier=1,
                           allow_small_or_imprecise_dtypes=True)
            nc.gpsimd.iota(k.spare_col[:], [[1, 1]], base=SPARE, channel_multiplier=1,
                           allow_small_or_imprecise_dtypes=True)
            nc.gpsimd.iota(k.iota_p[:], [[1, 1]], base=0, channel_multiplier=1,
                           allow_small_or_imprecise_dtypes=True)
            nc.gpsimd.memset(k.ones_f[:], 1.0)
            nc.gpsimd.memset(k.ident[:], 0.0)
            nc.gpsimd.memset(k.ident_b[:], 0.0)
            nc.gpsimd.memset(k.big_ident[:], 0.0)
            nc.gpsimd.memset(k.count_w[:], 1.0)
            nc.gpsimd.memset(k.eps[:], EPS)
            nc.gpsimd.memset(k.zero_b[:], 0.0)
            step(nc.gpsimd.memset(k.zero[:], 0.0))
            for t, v in ((k.ident, 1.0), (k.ident_b, 1.0), (k.big_ident, -BIG)):
                nc.gpsimd.affine_select(out=t[:], in_=t[:], compare_op=ALU.not_equal, fill=v, base=0,
                                        pattern=[[-1, P]], channel_multiplier=1)
            nc.gpsimd.affine_select(out=k.tri[:], in_=k.ones_f[:], compare_op=ALU.is_ge, fill=0.0, base=0,
                                    pattern=[[-1, P]], channel_multiplier=1)
            nc.gpsimd.affine_select(out=k.count_w[:], in_=k.count_w[:], compare_op=ALU.is_ge, fill=1025.0,
                                    base=-3 * P, pattern=[[1, 7 * P]], channel_multiplier=-1)
            nc.gpsimd.affine_select(out=k.below[:], in_=k.ones_f[:], compare_op=ALU.is_gt, fill=0.0, base=0,
                                    pattern=[[1, P]], channel_multiplier=-1)
            nc.gpsimd.memset(k.relations[:], 1.0)
            step(nc.gpsimd.memset(k.block_mask[:], 1.0))
            for cmp, base, sign in ((ALU.is_ge, 0, 1), (ALU.is_ge, 15, -1)):
                step(nc.gpsimd.affine_select(out=k.block_mask[:], in_=k.block_mask[:], compare_op=cmp, fill=0.0,
                                             base=base, pattern=[[-sign * 16, 8]], channel_multiplier=sign))
            for cmp, base in ((ALU.is_ge, 0), (ALU.is_ge, R - 1)):
                sign = 1 if base == 0 else -1
                step(nc.gpsimd.affine_select(out=k.relations[:], in_=k.relations[:], compare_op=cmp, fill=0.0,
                                             base=base, pattern=[[-sign * R, GN]], channel_multiplier=sign))

def edge_keys(nc, k):
    with Stage(nc) as c:
        def sb(name, shape, dt=F32):
            return c.enter_context(nc.sbuf_tensor(name, shape, dt))

        def sem(name):
            return c.semaphore(name)

        src_i = sb("src_i", [P, EC], I32)
        dst_i = sb("dst_i", [P, EC], I32)
        next_i = sb("next_i", [P, EC], I32)
        type_i = sb("type_i", [P, EC], I32)
        tmp_i = sb("tmp_i", [P, EC], I32)
        src_f = sb("src_f", [P, EC])
        dst_f = sb("dst_f", [P, EC])
        next_f = sb("next_f", [P, EC])
        type_f = sb("type_f", [P, EC])
        high = sb("high", [P, 98 * 8])
        low = sb("low", [P, 98 * 8])
        high_hot = sb("high_hot", [P, 98 * 8, 16], BF16)
        low_hot = sb("low_hot", [P, 98 * 8, 16], BF16)
        rec = sb("rec", [P, EC, 4])
        pair = sb("pair", [P, P])
        fold = sb("fold", [P, 16])
        count = sb("count", [16, 16])
        unsorted = sb("unsorted", [P, 1])
        pad_rec = sb("pad_rec", [P, 4])
        hist = c.enter_context(nc.psum_tensor("hist", [P, P], F32))
        folded = c.enter_context(nc.psum_tensor("folded", [P, 512], F32))
        loaded, key_step, hot_ready, hist_ready = sem("loaded"), sem("key_step"), sem("hot_ready"), sem("hist_ready")
        pair_ready, fold_ready, count_ready, rec_ready = (sem("pair_ready"), sem("fold_ready"), sem("count_ready"),
                                                          sem("rec_ready"))
        rec_written, count_written, unsorted_ready = sem("rec_written"), sem("count_written"), sem("unsorted_ready")
        fold_const = sem("fold_const")
        pad_step = sem("pad_step")
        block = c.enter_context(nc.Block())

        @block.sync
        def _(sp):
            sp.dma_start(dst_i[:], k.dst[0:EP].rearrange("(p j) -> p j", p=P)).then_inc(loaded, 16)
            sp.dma_start(src_i[:], k.src[0:EP].rearrange("(p j) -> p j", p=P)).then_inc(loaded, 16)
            sp.dma_start(type_i[:], k.type[0:EP].rearrange("(p j) -> p j", p=P)).then_inc(loaded, 16)
            sp.dma_start(next_i[:], k.dst[1:1 + EP].rearrange("(p j) -> p j", p=P)).then_inc(loaded, 16)
            for t in range(ZERO_FIRST):
                sp.dma_start(k.adj_rows[t * P:(t + 1) * P, :], k.zero[:, 0:NP]).then_inc(k.zero_written, 16)
            sp.dma_start(k.adj_spare, k.zero[:, 0:8]).then_inc(k.zero_written, 16)
            sp.wait_ge(rec_ready, 1)
            sp.dma_start(k.meta[0:EP, :].rearrange("(p j) c -> p j c", p=P), rec[:]).then_inc(rec_written, 16)
            sp.wait_ge(pad_step, 2)
            sp.dma_start(k.meta[EP:EP + P, :], pad_rec[:]).then_inc(rec_written, 16)
            sp.wait_ge(count_ready, 1)
            sp.dma_start(k.count_row.rearrange("(a b) -> a b", b=16), count[0:GW // 16, :]).then_inc(count_written, 16)
            sp.wait_ge(rec_written, 32)
            sp.wait_ge(count_written, 16)

        @block.gpsimd
        def _(pool):
            step = Steps(pool, pad_step)
            nc.gpsimd.memset(pad_rec[:], 0.0).then_inc(pad_step, 1)
            step.n = 1
            pool.wait_ge(pad_step, 1)
            step(nc.gpsimd.memset(pad_rec[:, 1:2], 1e6))
            nc.gpsimd.tensor_copy(fold[:], k.ident[:, 0:16]).then_inc(fold_const, 1)
            for j in range(1, 8):
                pool.wait_ge(fold_const, j)
                nc.gpsimd.tensor_add(fold[:], fold[:], k.ident[:, 16 * j:16 * j + 16]).then_inc(fold_const, 1)

        @block.vector
        def _(dve):
            step = Steps(dve, key_step)
            v = nc.vector
            dve.wait_ge(loaded, 64)
            step(v.tensor_single_scalar(tmp_i[:], dst_i[:], 4, ALU.arith_shift_right))
            step(v.tensor_copy(low[:, 0:EC], tmp_i[:]))
            step(v.tensor_single_scalar(tmp_i[:], dst_i[:], 8, ALU.arith_shift_right))
            v.memset(high[:, EC:], -1.0).then_inc(key_step, 1)
            step.n += 1
            step(v.tensor_copy(high[:, 0:EC], tmp_i[:]))
            v.memset(low[:, EC:], -1.0).then_inc(key_step, 1)
            step.n += 1
            step(v.scalar_tensor_tensor(low[:, 0:EC], high[:, 0:EC], -16.0, low[:, 0:EC], ALU.mult, ALU.add))
            v.tensor_tensor(high_hot[:], high[:].unsqueeze(2).to_broadcast([P, 784, 16]),
                            k.iota_row[:, 0:16].unsqueeze(1).to_broadcast([P, 784, 16]),
                            ALU.is_equal).then_inc(hot_ready, 1)
            v.tensor_tensor(low_hot[:], low[:].unsqueeze(2).to_broadcast([P, 784, 16]),
                            k.iota_row[:, 0:16].unsqueeze(1).to_broadcast([P, 784, 16]),
                            ALU.is_equal).then_inc(hot_ready, 1)
            v.tensor_copy(src_f[:], src_i[:]).then_inc(key_step, 1)
            v.tensor_copy(dst_f[:], dst_i[:]).then_inc(key_step, 1)
            v.tensor_copy(next_f[:], next_i[:]).then_inc(key_step, 1)
            step.n += 3
            step(v.tensor_copy(type_f[:], type_i[:]))
            v.scalar_tensor_tensor(rec[:, :, 0].bitcast(U32), src_f[:], float(R), type_f[:], ALU.mult,
                                   ALU.add).then_inc(key_step, 1)
            v.scalar_tensor_tensor(rec[:, :, 1], dst_f[:], float(R), type_f[:], ALU.mult,
                                   ALU.add).then_inc(key_step, 1)
            v.tensor_copy(rec[:, :, 2], src_f[:]).then_inc(key_step, 1)
            v.tensor_copy(rec[:, :, 3], dst_f[:]).then_inc(key_step, 1)
            v.scalar_tensor_tensor(k.adj_key[:, 0:EC], src_f[:], float(NP), dst_f[:], ALU.mult,
                                   ALU.add).then_inc(key_step, 1)
            step.n += 5
            step(v.tensor_copy(k.adj_key[:, EC:AE], k.trash_col[:, 7:8].to_broadcast([P, AE - EC])))
            v.tensor_copy(k.group_f[:], low[:, 0:EC]).then_inc(rec_ready, 1)
            step(v.tensor_tensor(next_f[:], dst_f[:], next_f[:], ALU.is_gt))
            step(v.tensor_reduce(unsorted[:], next_f[:], AX, ALU.add))
            dve.wait_ge(rec_ready, 1)
            step(v.scalar_tensor_tensor(k.group_f[:], high[:, 0:EC], 16.0, k.group_f[:], ALU.mult, ALU.add))
            dve.wait_ge(hist_ready, 1)
            step(v.tensor_copy(pair[:], hist[:]))
            for j in range(8):
                v.tensor_scalar(pair[:, 16 * j:16 * j + 16], pair[:, 16 * j:16 * j + 16],
                                k.block_mask[:, j:j + 1], None, ALU.mult).then_inc(pair_ready, 1)
            dve.wait_ge(fold_ready, 1)
            v.tensor_reduce(count[:], folded[0:16, 0:P].rearrange("a (j b) -> a b j", b=16), AX,
                            ALU.add).then_inc(count_ready, 1)
            dve.wait_ge(fold_ready, 2)
            v.tensor_copy(k.unsorted_i[:], folded[0:1, P:P + 1]).then_inc(unsorted_ready, 1)
            v.tensor_scalar(k.aside_i[:], folded[0:1, P:P + 1], 0.0, float(EP + P), ALU.is_gt,
                            ALU.mult).then_inc(unsorted_ready, 1)
            dve.wait_ge(unsorted_ready, 2)

        @block.tensor
        def _(pe):
            pe.wait_ge(hot_ready, 2)
            pe.matmul(hist[:], k.zero_b[:, 0:P], k.zero_b[:, 0:P], start=True, stop=False)
            with pe.Fori(0, 14) as j:
                for i in range(7):
                    pe.matmul(hist[:], high_hot[:].rearrange("p j a -> p (j a)")[:, bass.ds(j * (7 * P) + i * P, P)],
                              low_hot[:].rearrange("p j a -> p (j a)")[:, bass.ds(j * (7 * P) + i * P, P)],
                              start=False, stop=False, skip_group_check=True)
            pe.matmul(hist[:], k.zero_b[:, 0:P], k.zero_b[:, 0:P], start=False, stop=True).then_inc(hist_ready, 1)
            pe.wait_ge(pair_ready, 8)
            pe.wait_ge(fold_const, 8)
            pe.matmul(folded[0:16, 0:P], fold[:], pair[:], start=True, stop=True).then_inc(fold_ready, 1)
            pe.wait_ge(count_ready, 1)
            pe.matmul(folded[0:1, P:P + 1], k.ones_f[:, 0:1], unsorted[:], start=True, stop=True).then_inc(fold_ready, 1)

def schedule(nc, k):
    with Stage(nc) as c:
        def sb(name, shape, dt=F32):
            return c.enter_context(nc.sbuf_tensor(name, shape, dt))

        def sem(name):
            return c.semaphore(name)

        cnt = sb("cnt", [P, GW])
        cnt3 = sb("cnt3", [P, GW // 8])
        up_i = sb("up_i", [P, GW], I32)
        visits = sb("visits", [P, GW])
        ends = sb("ends", [P, GW])
        short = sb("short", [P, GW])
        zeros = sb("zeros", [P, GW])
        ones = sb("ones", [P, GW])
        scrap = sb("scrap", [P, GW])
        group = sb("group", [P, 2, B])
        off = sb("off", [P, 2, B])
        table_i = sb("table_i", [P, 4, B], I32)
        loaded, step_sem, ready, written = sem("sched_loaded"), sem("sched_step"), sem("table_ready"), sem("table_written")
        block = c.enter_context(nc.Block())

        @block.sync
        def _(sp):
            sp.dma_start(cnt[:], k.count_row.partition_broadcast(P)).then_inc(loaded, 16)
            for t in range(ZERO_FIRST, ZERO_NEXT):
                sp.dma_start(k.adj_rows[t * P:(t + 1) * P, :], k.zero[:, 0:NP]).then_inc(k.zero_written, 16)
            sp.wait_ge(ready, 1)
            for i in range(4):
                sp.dma_start(k.visit_i[i, :].rearrange("(p j) -> p j", p=P), table_i[:, i, :]).then_inc(written, 16)
            for i in range(2):
                sp.dma_start(k.visit_f[i, 1:1 + NV].rearrange("(p j) -> p j", p=P), group[:, i, :]).then_inc(written, 16)
            sp.dma_start(k.visit_f[:, 0:1], k.minus_one[0:2, :]).then_inc(written, 16)
            sp.wait_ge(written, 16 * 7)

        @block.vector
        def _(dve):
            step = Steps(dve, step_sem)
            v = nc.vector
            step(v.memset(zeros[:], 0.0))
            step(v.memset(k.minus_one[:], -1.0))
            step(v.memset(ones[:], 1.0))
            dve.wait_ge(loaded, 16)
            step(v.tensor_reduce(cnt3[:], cnt[:].rearrange("p (t g) -> p t g", g=8), AX, ALU.add))
            step(v.tensor_tensor_scan(k.starts[:], cnt[:], zeros[:], 0.0, ALU.add, ALU.add))
            step(v.tensor_tensor(k.starts[:], k.starts[:], cnt[:], ALU.subtract))
            for i, (counts, w) in enumerate(((cnt, GW), (cnt3, GW // 8))):
                step(v.tensor_scalar(visits[:, 0:w], counts[:], float(P - 1), None, ALU.add))
                step(v.tensor_copy(up_i[:, 0:w], visits[:, 0:w]))
                step(v.tensor_single_scalar(up_i[:, 0:w], up_i[:, 0:w], 7, ALU.arith_shift_right))
                step(v.tensor_copy(visits[:, 0:w], up_i[:, 0:w]))
                step(v.tensor_tensor_scan(ends[:, 0:w], visits[:, 0:w], zeros[:, 0:w], 0.0, ALU.add, ALU.add))
                step(v.scalar_tensor_tensor(short[:, 0:w], visits[:, 0:w], -float(P), counts[:], ALU.mult, ALU.add))
                for j in range(B):
                    step(v.scalar_tensor_tensor(scrap[:, 0:w], ends[:, 0:w], k.visit_col[:, j:j + 1], ones[:, 0:w],
                                                ALU.is_le, ALU.mult, accum_out=group[:, i, j:j + 1]))
                    step(v.scalar_tensor_tensor(scrap[:, 0:w], ends[:, 0:w], k.visit_col[:, j:j + 1], short[:, 0:w],
                                                ALU.is_le, ALU.mult, accum_out=off[:, i, j:j + 1]))
                step(v.scalar_tensor_tensor(off[:, i, :], k.visit_col[:], float(P), off[:, i, :], ALU.mult, ALU.add))
                step(v.tensor_scalar(off[:, i, :], off[:, i, :], float(EP), None, ALU.min))
                step(v.tensor_scalar(group[:, i, :], group[:, i, :], float(NG if i == 0 else NT), None, ALU.min))
                step(v.tensor_copy(table_i[:, 2 * i, :], off[:, i, :]))
                step(v.tensor_copy(table_i[:, 2 * i + 1, :], group[:, i, :]))
            v.tensor_copy(scrap[:, 0:1], zeros[:, 0:1]).then_inc(ready, 1)

def node_tables(nc, k):
    with Stage(nc) as c:
        def sb(name, shape, dt=F32):
            return c.enter_context(nc.sbuf_tensor(name, shape, dt))

        def sem(name):
            return c.semaphore(name)

        w_cat = sb("w_cat", [D, R * D])
        w_t = sb("w_t", [D, R * D])
        att = sb("att", [D, 2 * R])
        w_att = sb("w_att", [D, 2 * R])
        rows = sb("rows", [P, 2, R, TW])
        score = sb("score", [P, NT, 2, R])
        tab = sb("tab", [100, 2, 2, P])
        group_b = sb("group_b", [P, NV])
        prev_b = sb("prev_b", [P, NV])
        visit_hot = sb("visit_hot", [100, 2, NV])
        hundred = sb("hundred", [P, 2])
        h_ps = c.enter_context(nc.psum_tensor("h_ps", [P, 2, CW], F32))
        s_ps = c.enter_context(nc.psum_tensor("s_ps", [P, 2, CW], F32))
        v_ps = c.enter_context(nc.psum_tensor("v_ps", [P, 4, CW], F32))
        loaded, watt_ps, watt_ready = sem("tables_loaded"), sem("watt_ps"), sem("watt_ready")
        h_ready, h_copied, s_copied = sem("h_ready"), sem("h_copied"), sem("s_copied")
        row_written = [sem("row_written0"), sem("row_written1")]
        ones_ready, score_written, tab_loaded = sem("ones_ready"), sem("score_written"), sem("tab_loaded")
        hot_step, by_visit_ready, by_visit_copied = sem("hot_step"), sem("by_visit_ready"), sem("by_visit_copied")
        v_loaded = sem("v_loaded")
        block = c.enter_context(nc.Block())

        @block.sync
        def _(sp):
            for dst, src in ((w_cat[:], k.w_cat), (w_t[:], k.w_t), (att[:, 0:R], k.att_src), (att[:, R:2 * R], k.att_dst),
                             (k.x_t[:], k.x_cols), (k.x_n[:], k.x_rows.rearrange("(t p) d -> p t d", p=P))):
                sp.dma_start(dst, src).then_inc(loaded, 16)
            sp.dma_start(group_b[:], k.visit_f[0, 1:1 + NV].partition_broadcast(P)).then_inc(v_loaded, 16)
            sp.dma_start(prev_b[:], k.visit_f[0, 0:NV].partition_broadcast(P)).then_inc(v_loaded, 16)
            sp.dma_start(k.tile_f[:], k.visit_f[1, 1:1 + NV].partition_broadcast(P)).then_inc(v_loaded, 16)
            sp.dma_start(k.visit_row[:], k.visit_i.rearrange("(a i) c -> a i c", a=1)).then_inc(v_loaded, 16)
            for t in range(NT):
                sp.wait_ge(h_copied, t + 1)
                sp.wait_ge(s_copied, t + 1)
                sp.dma_start(k.table[t * P * R:(t + 1) * P * R, :].rearrange("(p r) f -> p (r f)", r=R),
                             rows[:, t % 2].rearrange("p r f -> p (r f)")).then_inc(row_written[t % 2], 16)
                z, h = ZERO_NEXT + t // 2, (t % 2) * (NP // 2)
                if z < NT:
                    sp.dma_start(k.adj_rows[z * P:(z + 1) * P, h:h + NP // 2], k.zero[:, 0:NP // 2]
                                 ).then_inc(k.zero_written, 16)
            for w in range(2):
                sp.dma_start(k.score_row[w].rearrange("(t p r) -> p t r", p=P, r=R),
                             score[:, :, w, :]).then_inc(score_written, 16)
            sp.wait_ge(score_written, 32)
            for w in range(2):
                sp.dma_start(tab[:, w], k.score_row[w].rearrange("(a g n) -> g a n", a=2, n=P)).then_inc(tab_loaded, 16)
            sp.wait_ge(row_written[0], 16 * ((NT + 1) // 2))
            sp.wait_ge(row_written[1], 16 * (NT // 2))

        @block.tensor
        def _(pe):
            pe.wait_ge(loaded, 96)
            for w in range(2):
                for r in range(R):
                    m = pe.matmul(v_ps[0:D, 0, w * R + r:w * R + r + 1], w_t[:, r * D:(r + 1) * D],
                                  att[:, w * R + r:w * R + r + 1], start=True, stop=True)
            m.then_inc(watt_ps, 1)
            pe.wait_ge(watt_ready, 1)
            for t in range(NT):
                if t >= 2:
                    pe.wait_ge(h_copied, t - 1)
                    pe.wait_ge(s_copied, t - 1)
                pe.matmul(h_ps[:, t % 2, :], k.x_t[:, t * P:(t + 1) * P], w_cat[:], start=True, stop=True)
                pe.matmul(s_ps[:, t % 2, 0:2 * R], k.x_t[:, t * P:(t + 1) * P], w_att[:], start=True,
                          stop=True).then_inc(h_ready, 1)
            pe.wait_ge(tab_loaded, 32)
            pe.wait_ge(hot_step, 6)
            for w in range(2):
                for i in range(2):
                    for a in range(2):
                        m = pe.matmul(v_ps[:, 2 * w + i, :], tab[:, w, a, :], visit_hot[:, a, i * CW:(i + 1) * CW],
                                      start=(a == 0), stop=(a == 1))
            m.then_inc(by_visit_ready, 1)

        @block.scalar
        def _(act):
            for t in range(NT):
                act.wait_ge(h_ready, t + 1)
                if t >= 2:
                    act.wait_ge(row_written[t % 2], 16 * (t // 2))
                nc.scalar.copy(rows[:, t % 2, :, 0:D], h_ps[:, t % 2, :].rearrange("p (r f) -> p r f", r=R)).then_inc(h_copied, 1)

        @block.vector
        def _(dve):
            v = nc.vector
            step = Steps(dve, hot_step)
            v.memset(rows[:, :, :, D:D + 1], 1.0).then_inc(ones_ready, 1)
            dve.wait_ge(watt_ps, 1)
            v.tensor_copy(w_att[:], v_ps[0:D, 0, 0:2 * R]).then_inc(watt_ready, 1)
            for t in range(NT):
                dve.wait_ge(h_ready, t + 1)
                if t >= 2:
                    dve.wait_ge(row_written[t % 2], 16 * (t // 2))
                v.tensor_copy(score[:, t], s_ps[:, t % 2, 0:2 * R].rearrange("p (w r) -> p w r", w=2)).then_inc(ones_ready, 1)
                v.tensor_copy(rows[:, t % 2, :, D + 1:TW],
                              s_ps[:, t % 2, 0:R].unsqueeze(2)).then_inc(s_copied, 1)
            dve.wait_ge(v_loaded, 64)
            step(v.tensor_scalar(hundred[:, 0:1], k.iota_p[:], 0.0, None, ALU.add))
            step(v.tensor_scalar(hundred[:, 1:2], k.iota_p[:], 100.0, None, ALU.add))
            for a in range(2):
                step(v.tensor_scalar(visit_hot[:, a, :], group_b[0:100, :], hundred[0:100, a:a + 1], None, ALU.is_equal))
            step(v.tensor_tensor(k.fresh[:], group_b[:], prev_b[:], ALU.not_equal))
            step(v.tensor_scalar(k.fresh[:], k.fresh[:], -BIG, None, ALU.mult))
            step(v.tensor_scalar(k.key_base[:], group_b[:], float(P), None, ALU.mult))
            step(v.tensor_scalar(k.tile_base[:], k.tile_f[:], float(P), None, ALU.mult))
            dve.wait_ge(by_visit_ready, 1)
            v.tensor_copy(k.self_v[:], v_ps[:, 0:2, :].rearrange("p i c -> p (i c)")).then_inc(by_visit_copied, 1)
            v.tensor_copy(k.dst_v[:], v_ps[:, 2:4, :].rearrange("p i c -> p (i c)")).then_inc(by_visit_copied, 1)
            dve.wait_ge(by_visit_copied, 2)

def group_records(nc, k):
    with Stage(nc) as c:
        def sb(name, shape, dt=F32):
            return c.enter_context(nc.sbuf_tensor(f"gr_{name}", shape, dt))

        def sem(name):
            return c.semaphore(f"gr_{name}")

        iota_group = sb("iota_group", [P, GW])
        below = sb("below", [P, P], BF16)
        ones = sb("ones", [P, P], BF16)
        next_place = sb("next_place", [P, GW])
        hot = sb("hot", [P, GW], BF16)
        places = sb("places", [P, GW])
        scrap = sb("scrap", [P, GW])
        place = sb("place", [P, 1])
        place_i = sb("place_i", [P, 1], U32)
        rec = sb("rec", [P, RW])
        before = c.enter_context(nc.psum_tensor("gr_before", [P, CW], F32))
        column = c.enter_context(nc.psum_tensor("gr_column", [P, CW], F32))
        copied, masks_ready, step_sem, hot_ready = sem("copied"), sem("masks_ready"), sem("step"), sem("hot_ready")
        counted, place_ready, loaded, placed = sem("counted"), sem("place_ready"), sem("loaded"), sem("placed")
        passed, skipped, tail_copied = sem("passed"), sem("skipped"), sem("tail_copied")
        block = c.enter_context(nc.Block())

        def disorder(engine):
            return nc.values_load_multi_w_load_instructions(
                k.unsorted_i[0:1, 0:1], engines=[engine], min_val=0, max_val=EP,
                skip_runtime_bounds_check_because="a number of edges")[1][0]

        @block.sync
        def _(sp):
            with sp.If(disorder(mybir.EngineType.SP) > 0):
                sp.dma_start(k.meta_copy, k.meta[0:EP, :]).then_inc(copied, 16)
                sp.dma_start(k.rec[EP:EP + P, 0:4], k.meta[EP:EP + P, :]).then_inc(tail_copied, 16)
                sp.dma_start(k.rec[EP:EP + P, 4:RW], k.edge_attr[EP:EP + P, :]).then_inc(tail_copied, 16)
                sp.wait_ge(tail_copied, 32)
                sp.wait_ge(copied, 16)
                meta = k.meta_copy.rearrange("(p j) c -> p (j c)", p=P)
                features = k.edge_attr[0:EP, :].rearrange("(p j) c -> p (j c)", p=P)
                sp.dma_start(rec[:, 0:4], meta[:, 0:4]).then_inc(loaded, 16)
                sp.dma_start(rec[:, 4:RW], features[:, 0:D]).then_inc(loaded, 16)
                with sp.Fori(1, EC) as j:
                    sp.wait_ge(placed, j * 32)
                    sp.dma_start(rec[:, 0:4], meta[:, bass.ds(j * 4, 4)]).then_inc(loaded, 16)
                    sp.dma_start(rec[:, 4:RW], features[:, bass.ds(j * D, D)]).then_inc(loaded, 16)
            with sp.Else():
                sp.sem_inc(skipped, 1)

        @block.gpsimd
        def _(pool):
            with pool.If(disorder(mybir.EngineType.Pool) > 0):
                nc.gpsimd.iota(iota_group[:], [[1, GW]], base=0, channel_multiplier=0,
                               allow_small_or_imprecise_dtypes=True).then_inc(masks_ready, 1)
                nc.gpsimd.tensor_copy(ones[:], k.ones_f[:]).then_inc(masks_ready, 1)
                nc.gpsimd.tensor_copy(below[:], k.below[:]).then_inc(masks_ready, 1)
                with pool.Fori(0, EC) as j:
                    pool.wait_ge(loaded, j * 32 + 32)
                    pool.wait_ge(place_ready, j + 1)
                    pool.sem_inc(passed, 1)
                    pool.indirect_dma_start(k.rec, bass.IndirectOffsetOnAxis(place_i[:, 0:1], 0), rec[:], None
                                            ).then_inc(placed, 16)
                    pool.indirect_dma_start(k.meta, bass.IndirectOffsetOnAxis(place_i[:, 0:1], 0), rec[:, 0:4], None
                                            ).then_inc(placed, 16)
                pool.wait_ge(placed, 32 * EC)
            with pool.Else():
                pool.sem_inc(skipped, 1)

        @block.tensor
        def _(pe):
            with pe.If(disorder(mybir.EngineType.PE) > 0):
                pe.wait_ge(masks_ready, 3)
                with pe.Fori(0, EC) as j:
                    pe.wait_ge(hot_ready, j + 1)
                    pe.matmul(before[:, 0:GW], below[:], hot[:], start=True, stop=True)
                    pe.matmul(column[:, 0:GW], ones[:], hot[:], start=True, stop=True).then_inc(counted, 1)
            with pe.Else():
                pe.sem_inc(skipped, 1)

        @block.vector
        def _(dve):
            v = nc.vector
            ch = Chain(dve, step_sem)
            steps = 3

            def body(j, first):
                ch.wait()
                v.tensor_tensor(hot[:], k.group_f[:, bass.ds(j, 1)].to_broadcast([P, GW]), iota_group[:],
                                ALU.is_equal).then_inc(hot_ready, 1)
                dve.wait_ge(counted, j + 1)
                ch.step(v.tensor_tensor(places[:], before[:, 0:GW], next_place[:], ALU.add))
                ch(v.scalar_tensor_tensor(scrap[:], places[:], 1.0, hot[:], ALU.mult, ALU.mult, accum_out=place[:]))
                ch.step(v.tensor_tensor(next_place[:], column[:, 0:GW], next_place[:], ALU.add))
                if not first:
                    dve.wait_ge(placed, j * 32)
                v.tensor_copy(place_i[:], place[:]).then_inc(place_ready, 1)

            with dve.If(disorder(mybir.EngineType.DVE) > 0):
                v.tensor_copy(next_place[:], k.starts[:]).then_inc(step_sem, 1)
                dve.wait_ge(masks_ready, 3)
                ch.begin(1)
                body(0, True)
                with dve.Fori(1, EC) as j:
                    ch.begin(j * steps + 1)
                    body(j, False)
            with dve.Else():
                dve.sem_inc(skipped, 1)

class Chain:

    def __init__(self, eng, sem):
        self.eng, self.sem, self.base, self.n = eng, sem, 0, 0

    def begin(self, base):
        self.base, self.n = base, 0

    def __call__(self, ins):
        self.n += 1
        ins.then_inc(self.sem, 1)

    def wait(self, back=0):
        self.eng.wait_ge(self.sem, self.base + (self.n - back))

    def step(self, ins):
        self(ins)
        self.wait()

def attention(nc, k):
    with Stage(nc) as c:
        def sb(name, shape, dt=F32):
            return c.enter_context(nc.sbuf_tensor(name, shape, dt))

        def ps(name, shape, dt=F32):
            return c.enter_context(nc.psum_tensor(name, shape, dt))

        def sem(name):
            return c.semaphore(name)

        rec = sb("rec_s", [P, 2, B, 4])
        hs = sb("hs", [P, 2, B, TW])
        key = sb("key", [P, 2, B])
        miss = sb("miss", [P, 2, B, P], BF16)
        hit = sb("hit", [P, 2, B, P])
        hit_t = sb("hit_t", [P, 2, B, P])
        top = sb("top", [P, 2, B])
        run = sb("run", [P, 2, B + 1])
        old = sb("old", [P, 2, B])
        logit = sb("logit", [P, 2, 2, B])
        lrelu = sb("lrelu", [P, 2, 2, B])
        fade_in = sb("fade_in", [P, 2, B])
        fade = sb("fade", [P, 2, B])
        pick = sb("pick", [P, 2, B, 2])
        zed = sb("zed", [P, 2, B])
        lz = sb("lz", [P, 2, B])
        weight = sb("weight", [P, 2, B])
        hw = sb("hw", [P, 2, B, TW])
        AS = (AC + 1) // 2
        akey = sb("akey", [P, 2, AS])
        same = sb("same", [P, 2, AS, 4 * P])
        seen = sb("seen", [P, 2, AS])
        later = sb("later", [P, 2, AS])
        gap = sb("gap", [P, 2, AS])
        aidx = sb("aidx", [P, 2, AS], U32)
        miss_t = ps("miss_t", [P, B, P], BF16)
        masked = ps("masked", [P, B, P])
        picked = ps("picked", [P, CW])
        sums = ps("sums_ps", [P, 2, CW])
        akey_t = ps("akey_t", [P, 2, 4, P])

        rec_loaded = [sem(f"rec_loaded{s}") for s in range(2)]
        gathered = [sem(f"gathered{s}") for s in range(2)]
        step_sem, key_used, miss_ready, hit_ready = sem("attn_step"), sem("key_used"), sem("miss_ready"), sem("hit_ready")
        miss_t_ready, hit_t_ready, masked_ready = sem("miss_t_ready"), sem("hit_t_ready"), sem("masked_ready")
        fade_asked, fade_ready, pick_ready, picked_ready = (sem("fade_asked"), sem("fade_ready"), sem("pick_ready"),
                                                            sem("picked_ready"))
        weight_asked, weight_ready, hw_ready, sums_ready = (sem("weight_asked"), sem("weight_ready"), sem("hw_ready"),
                                                            sem("sums_ready"))
        top_ready, acc_done = sem("top_ready"), sem("acc_done")
        akey_ready, akey_t_ready, aidx_ready, added, seen_ready = (sem("akey_ready"), sem("akey_t_ready"),
                                                                   sem("aidx_ready"), sem("added"), sem("seen_ready"))
        run_start, passed = sem("run_start"), sem("passed")
        acc_loaded, sums_zeroed, rec_written = sem("acc_loaded"), sem("sums_zeroed"), sem("records_written")
        block = c.enter_context(nc.Block())
        half = [AS, AC - AS]
        IT = NB0 // 2

        @block.sync
        def _(sp):
            def body(it, first):
                for s in range(2):
                    _, offs = nc.values_load_multi_w_load_instructions(
                        k.visit_row[0:1, 0, bass.ds(it * (2 * B) + s * B, B)], engines=[mybir.EngineType.SP],
                        min_val=0, max_val=EP, skip_runtime_bounds_check_because="clamped to the table's end")
                    if not first:
                        sp.wait_ge(gathered[s], it * (16 * B))
                        sp.wait_ge(key_used, it * 2 + (s - 1))
                    for u in range(B):
                        sp.dma_start(rec[:, s, u, :], k.meta[bass.ds(offs[u], P), :]).then_inc(rec_loaded[s], 16)
            def records(it, rows):
                aside = nc.values_load_multi_w_load_instructions(
                    k.aside_i[0:1, 0:1], engines=[mybir.EngineType.SP], min_val=0, max_val=EP + P,
                    skip_runtime_bounds_check_because="0 or EP + P")[1][0]
                to = bass.ds(aside + it * CR, rows)
                sp.dma_start(k.rec[to, 0:4], k.meta[bass.ds(it * CR, rows), :]).then_inc(rec_written, 16)
                sp.dma_start(k.rec[to, 4:RW], k.edge_attr[bass.ds(it * CR, rows), :]).then_inc(rec_written, 16)

            body(0, True)
            sp.dma_start(k.acc[:], k.table[0:(NG + 1) * P, :].rearrange("(g k) f -> k g f", k=P)).then_inc(acc_loaded, 16)
            with sp.Fori(1, IT) as it:
                body(it, False)
                records(it - 1, CR)
            for a in range(NACC):
                sp.dma_start(k.sums_flat[a].rearrange("(p r) h -> p (r h)", p=P), k.zero[:]).then_inc(sums_zeroed, 16)
            records(IT - 1, EP + P - (IT - 1) * CR)
            sp.wait_ge(rec_written, 32 * IT)
            sp.wait_ge(sums_zeroed, 16 * NACC)

        @block.gpsimd
        def _(pool):
            def body(it, first):
                for s in range(2):
                    pool.wait_ge(rec_loaded[s], it * (16 * B) + 16 * B)
                    if not first:
                        pool.wait_ge(hw_ready, it * 2 + (s - 1))
                    pool.sem_inc(passed, 1)
                    for u in range(B):
                        pool.indirect_dma_start(hs[:, s, u, :], None, k.table,
                                                bass.IndirectOffsetOnAxis(rec[:, s, u, 0:1].bitcast(U32), 0)
                                                ).then_inc(gathered[s], 16)
                        if u % 4 == 3:
                            a0 = 4 * (u // 4)
                            if u == 3:
                                pool.wait_ge(aidx_ready, it * 2 + (s + 1))
                            done = s * half[0] + a0
                            if done or not first:
                                pool.wait_ge(added, it * (16 * AC) + 16 * done)
                            pool.sem_inc(passed, 1)
                            for a in range(a0, min(a0 + 4, half[s])):
                                pool.indirect_dma_start(k.adj, bass.IndirectOffsetOnAxis(aidx[:, s, a:a + 1], 0),
                                                        seen[:, s, a:a + 1], None, compute_op=ALU.add).then_inc(added, 16)
            pool.wait_ge(k.zero_written, 16 * k.zero_dmas)
            body(0, True)
            with pool.Fori(1, IT) as it:
                body(it, False)
            pool.wait_ge(added, 16 * AE)

        @block.scalar
        def _(act):
            def masks_t(m, first):
                act.wait_ge(miss_t_ready, m + 1)
                if not first:
                    act.wait_ge(picked_ready, m - 1)
                nc.scalar.activation(hit_t[:, m_slot[0]], miss_t[:], ACT.Identity, bias=k.ones_f[:, 0:1],
                                     scale=-1.0).then_inc(hit_t_ready, 1)

            def masks(m, first):
                act.wait_ge(miss_ready, m + 1)
                if not first:
                    act.wait_ge(sums_ready, m - 1)
                nc.scalar.activation(hit[:, m_slot[0]], miss[:, m_slot[0]], ACT.Identity, bias=k.ones_f[:, 0:1],
                                     scale=-1.0).then_inc(hit_ready, 1)

            m_slot = [0]

            def body(it, last):
                for s in range(2):
                    n1 = it * 2 + (s + 1)
                    act.wait_ge(fade_asked, n1)
                    nc.scalar.activation(fade[:, s], fade_in[:, s], ACT.Exp).then_inc(fade_ready, 1)
                    act.wait_ge(weight_asked, n1)
                    nc.scalar.activation(weight[:, s], lz[:, s], ACT.Exp).then_inc(weight_ready, 1)
                    if not last:
                        m_slot[0] = s
                        masks_t(it * 2 + (s + 2), False)
                        masks(it * 2 + (s + 2), False)

            for s in range(2):
                m_slot[0] = s
                masks_t(s, True)
                masks(s, True)
            with act.Fori(0, IT - 1) as it:
                body(it, False)
            body(IT - 1, True)

        @block.tensor
        def _(pe):
            def keys_t(m, s, first):
                pe.wait_ge(akey_ready, m + 1)
                if not first:
                    pe.wait_ge(seen_ready, m)
                for u in range(half[s]):
                    t = pe.transpose(akey_t[:, u // 4, u % 4, :], akey[:, s, u:u + 1].to_broadcast([P, P]), k.ident[:])
                t.then_inc(akey_t_ready, 1)

            def masks_t(m, s, first):
                pe.wait_ge(miss_ready, m + 1)
                if not first:
                    pe.wait_ge(hit_t_ready, m)
                for u in range(B):
                    t = pe.transpose(miss_t[:, u, :], miss[:, s, u, :], k.ident_b[:])
                t.then_inc(miss_t_ready, 1)

            def scores(m, s, rows, first):
                pe.wait_ge(gathered[s], rows)
                if not first:
                    pe.wait_ge(top_ready, m)
                for u in range(B):
                    pe.matmul(masked[:, u, :], miss[:, s, u, :], k.big_ident[:], start=True, stop=False)
                    t = pe.matmul(masked[:, u, :], hs[:, s, u, D + 1:D + 2].to_broadcast([P, P]), k.ident[:],
                                  start=False, stop=True)
                t.then_inc(masked_ready, 1)

            def body(it, first, last):
                for s in range(2):
                    n1 = it * 2 + (s + 1)
                    if not last:
                        keys_t(it * 2 + (s + 2), s, False)
                    pe.wait_ge(pick_ready, n1)
                    pe.wait_ge(hit_t_ready, n1)
                    for u in range(B):
                        m = pe.matmul(picked[:, 2 * u:2 * u + 2], hit_t[:, s, u, :], pick[:, s, u, :], start=True, stop=True)
                    m.then_inc(picked_ready, 1)
                    if not (last and s == 1):
                        scores(it * 2 + (s + 1), 1 - s, it * (16 * B) + 16 * B * (s + 1), False)
                    if not last:
                        masks_t(it * 2 + (s + 2), s, False)
                    pe.wait_ge(hw_ready, n1)
                    pe.wait_ge(hit_ready, n1)
                    if not (first and s == 0):
                        pe.wait_ge(acc_done, it * 2 + s)
                    for u in range(B):
                        m = pe.matmul(sums[:, u // 4, (u % 4) * TW:(u % 4 + 1) * TW], hit[:, s, u, :], hw[:, s, u, :],
                                      start=True, stop=True)
                    m.then_inc(sums_ready, 1)

            for s in range(2):
                keys_t(s, s, s == 0)
                masks_t(s, s, s == 0)
            scores(0, 0, 16 * B, True)
            body(0, True, False)
            with pe.Fori(1, IT - 1) as it:
                body(it, False, False)
            body(IT - 1, False, True)

        @block.vector
        def _(dve):
            v = nc.vector
            ch = Chain(dve, step_sem)

            def groups_of(it, s):
                return nc.values_load_multi_w_load_instructions(
                    k.visit_row[0:1, 1, bass.ds(it * (2 * B) + s * B, B)], engines=[mybir.EngineType.DVE],
                    min_val=0, max_val=NG, skip_runtime_bounds_check_because="clamped to the spare group")[1]

            def update(groups, s, u, n1):
                a = k.acc[:, bass.ds(groups[u], 1), :].rearrange("p g f -> p (g f)")
                ins = v.scalar_tensor_tensor(a, a, fade[:, s, u:u + 1],
                                             sums[:, u // 4, (u % 4) * TW:(u % 4 + 1) * TW], ALU.mult, ALU.add)
                if u == B - 1:
                    ins.then_inc(acc_done, 1)
                else:
                    ch(ins)

            def keys(it, s, first):
                if not first:
                    dve.wait_ge(added, it * (16 * AC) + 16 * (half[0] - AC) * (1 - s))
                v.tensor_tensor(akey[:, s, 0:half[s]], k.adj_key[:, bass.ds(it * AC + s * half[0], half[s])],
                                k.zero_f[:, 0:half[s]], ALU.add).then_inc(akey_ready, 1)

            def compare(s, u):
                q, w0 = u // 4, 3 - u % 4
                wide = min(4, half[s] - 4 * q) * P
                return v.scalar_tensor_tensor(same[:, s, u, 0:wide],
                                              akey_t[:, q].rearrange("p u e -> p (u e)")[:, 0:wide],
                                              akey[:, s, u:u + 1], k.count_w[:, w0 * P:w0 * P + wide],
                                              ALU.is_equal, ALU.mult, accum_out=seen[:, s, u:u + 1])

            def entries(s, n1):
                w = half[s]
                dve.wait_ge(seen_ready, n1)
                ch(v.tensor_scalar(later[:, s, 0:w], seen[:, s, 0:w], 1024.0, None, ALU.is_ge))
                ch.step(v.tensor_tensor(gap[:, s, 0:w], k.trash_col[:, 0:w], akey[:, s, 0:w], ALU.subtract))
                ch.step(v.tensor_tensor(gap[:, s, 0:w], gap[:, s, 0:w], later[:, s, 0:w], ALU.mult))
                v.tensor_tensor(aidx[:, s, 0:w], gap[:, s, 0:w], akey[:, s, 0:w], ALU.add).then_inc(aidx_ready, 1)

            def masks(it, s, n1, first=False):
                if not first:
                    dve.wait_ge(hit_ready, n1 - 2)
                dve.wait_ge(rec_loaded[s], it * (16 * B) + 16 * B)
                v.tensor_tensor(key[:, s], rec[:, s, :, 1], k.key_base[:, bass.ds(it * (2 * B) + s * B, B)],
                                ALU.subtract).then_inc(key_used, 1)
                dve.wait_ge(key_used, n1)
                v.tensor_tensor(miss[:, s], key[:, s].unsqueeze(2).to_broadcast([P, B, P]),
                                k.iota_row[:].unsqueeze(1).to_broadcast([P, B, P]), ALU.not_equal).then_inc(miss_ready, 1)

            def maxima(it, s, n1):
                w = 1 - s
                vis = bass.ds(it * (2 * B) + s * B, B)
                dve.wait_ge(masked_ready, n1)
                v.tensor_reduce(top[:, s], masked[:], AX, ALU.max).then_inc(top_ready, 1)
                ch(v.tensor_copy(run[:, s, 0:1], run[:, w, B:B + 1]))
                ch(v.tensor_tensor(pick[:, s, :, 0], k.dst_v[:, vis], k.zero_f[:, 0:B], ALU.add))
                dve.wait_ge(top_ready, n1)
                ch.step(v.tensor_tensor(top[:, s], top[:, s], k.self_v[:, vis], ALU.max))
                ch.step(v.tensor_tensor_scan(run[:, s, 1:B + 1], k.fresh[:, vis], top[:, s], run[:, w, B:B + 1],
                                             ALU.add, ALU.max))
                ch(v.tensor_tensor(logit[:, s, 0], run[:, s, 1:B + 1], k.dst_v[:, vis], ALU.add))
                ch.step(v.tensor_tensor(old[:, s], run[:, s, 0:B], k.fresh[:, vis], ALU.add))
                ch.step(v.tensor_tensor(old[:, s], old[:, s], k.self_v[:, vis], ALU.max))
                ch.step(v.tensor_tensor(logit[:, s, 1], old[:, s], k.dst_v[:, vis], ALU.add))
                ch.step(v.scalar_tensor_tensor(lrelu[:, s], logit[:, s], SLOPE, logit[:, s], ALU.mult, ALU.max))
                v.tensor_copy(pick[:, s, :, 1], lrelu[:, s, 0]).then_inc(pick_ready, 1)
                v.tensor_tensor(fade_in[:, s], lrelu[:, s, 1], lrelu[:, s, 0], ALU.subtract).then_inc(fade_asked, 1)

            def body(it, first, last):
                for s in range(2):
                    n1 = it * 2 + (s + 1)
                    before = not (first and s == 0)
                    if not last:
                        keys(it + 1, s, False)
                    maxima(it, s, n1)
                    if not last:
                        masks(it + 1, s, n1 + 2)
                        dve.wait_ge(akey_t_ready, n1 + 2)
                        compare(s, 0)
                    dve.wait_ge(picked_ready, n1)
                    pair = picked[:, 0:2 * B].rearrange("p (u w) -> p u w", w=2)
                    ch.step(v.tensor_tensor(zed[:, s], hs[:, s, :, D + 1], pair[:, :, 0], ALU.add))
                    ch.step(v.scalar_tensor_tensor(zed[:, s], zed[:, s], SLOPE, zed[:, s], ALU.mult, ALU.max))
                    ch.step(v.tensor_tensor(zed[:, s], zed[:, s], pair[:, :, 1], ALU.subtract))
                    v.tensor_scalar(lz[:, s], zed[:, s], 0.0, None, ALU.min).then_inc(weight_asked, 1)
                    if not last:
                        compare(s, 1)
                    dve.wait_ge(weight_ready, n1)
                    v.tensor_tensor(hw[:, s], hs[:, s], weight[:, s].unsqueeze(2).to_broadcast([P, B, TW]),
                                    ALU.mult).then_inc(hw_ready, 1)
                    if first and s == 1:
                        dve.wait_ge(acc_loaded, 16)
                    if before:
                        groups = groups_of(it if s == 1 else it - 1, 1 - s)
                        dve.wait_ge(sums_ready, n1 - 1)
                    for u in range(B):
                        if before:
                            if u:
                                ch.wait()
                            update(groups, 1 - s, u, n1)
                        if not last and u + 2 < half[s]:
                            ins = compare(s, u + 2)
                    if not last:
                        ins.then_inc(seen_ready, 1)
                        entries(s, n1 + 2)
                    if before:
                        dve.wait_ge(acc_done, n1 - 1)

            v.memset(k.zero_f[:], 0.0).then_inc(run_start, 1)
            v.memset(run[:, 1, B:B + 1], -BIG).then_inc(run_start, 1)
            dve.wait_ge(run_start, 2)
            ch.begin(0)
            for s in range(2):
                keys(0, s, True)
                masks(0, s, s + 1, True)
                dve.wait_ge(akey_t_ready, s + 1)
                for u in range(half[s]):
                    ins = compare(s, u)
                ins.then_inc(seen_ready, 1)
                entries(s, s + 1)
            body(0, True, False)
            start, steps = ch.n, 2 * (B - 1 + 3 + 9 + 3)
            with dve.Fori(1, IT - 1) as it:
                ch.begin((it - 1) * steps + start)
                body(it, False, False)
                assert ch.n == steps, ch.n
            ch.begin((IT - 2) * steps + start)
            body(IT - 1, False, True)
            groups = groups_of(IT - 1, 1)
            dve.wait_ge(sums_ready, NB0)
            for u in range(B):
                if u:
                    ch.wait()
                update(groups, 1, u, NB0)
            dve.wait_ge(acc_done, NB0)

def finish_attention(nc, k):
    with Stage(nc) as c:
        def sb(name, shape, dt=F32):
            return c.enter_context(nc.sbuf_tensor(name, shape, dt))

        def sem(name):
            return c.semaphore(name)

        inv = sb("inv", [P, NG - 1])
        w_self = sb("w_self", [D, D])
        biases = sb("biases", [R + 1, D])
        bias_sum = sb("bias_sum", [P, D])
        by_group = sb("by_group", [GN, NT, 8, D])
        summed = sb("att_summed", [P, NT, D])
        self_ps = c.enter_context(nc.psum_tensor("self_ps", [P, 4, CW], F32))
        group_ps = c.enter_context(nc.psum_tensor("group_ps", [P, 3, CW], F32))
        bias_ps = c.enter_context(nc.psum_tensor("bias_ps", [P, CW], F32))
        loaded, fin_step, scaled, self_ready = sem("fin_loaded"), sem("fin_step"), sem("fin_scaled"), sem("self_ready")
        group_ready, group_copied, cleared = sem("group_ready"), sem("group_copied"), sem("by_group_cleared")
        moved = [sem("moved0"), sem("moved1")]
        block = c.enter_context(nc.Block())
        groups = NG - 1
        per = 8
        halves = ((0, 13), (13, NT))

        @block.sync
        def _(sp):
            sp.dma_start(w_self[:], k.w_self0).then_inc(loaded, 16)
            sp.dma_start(biases[:], k.bias0).then_inc(loaded, 16)
            sp.wait_ge(cleared, 1)
            for i, (a, b) in enumerate(halves):
                sp.wait_ge(group_copied, b)
                for j in range(8):
                    sp.dma_start(summed[j * GN:(j + 1) * GN, a:b, :], by_group[:, a:b, j, :]).then_inc(moved[i], 16)

        @block.vector
        def _(dve):
            v = nc.vector
            step = Steps(dve, fin_step)
            v.memset(by_group[:, NT - 1], 0.0).then_inc(cleared, 1)
            step(v.reciprocal(inv[:], k.acc[:, 0:groups, D]))
            for t in range(NT):
                a, b = t * per, min(t * per + per, groups)
                v.tensor_tensor(k.acc[:, a:b, 0:D], k.acc[:, a:b, 0:D],
                                inv[:, a:b].unsqueeze(2).to_broadcast([P, b - a, D]), ALU.mult).then_inc(scaled, 1)
            dve.wait_ge(self_ready, NT + 1)
            step(v.tensor_copy(bias_sum[:], bias_ps[:, 0:D]))
            for q in range(4):
                t0, t1 = q * per, min(q * per + per, NT)
                v.tensor_tensor(k.pre[:, t0:t1, :], k.x_n[:, t0:t1, :],
                                self_ps[:, q, 0:(t1 - t0) * D].rearrange("p (t d) -> p t d", d=D),
                                ALU.add).then_inc(fin_step, 1)
            step.n += 4
            dve.wait_ge(fin_step, step.n)
            step(v.tensor_tensor(k.pre[:], k.pre[:], bias_sum[:].unsqueeze(1).to_broadcast([P, NT, D]), ALU.add))
            for i, (a, b) in enumerate(halves):
                dve.wait_ge(moved[i], 16 * 8)
                step(v.tensor_tensor(k.pre[:, a:b], k.pre[:, a:b], summed[:, a:b], ALU.add))

        @block.tensor
        def _(pe):
            pe.wait_ge(loaded, 32)
            pe.matmul(bias_ps[:, 0:D], k.ones_f[0:R + 1, :], biases[:], start=True, stop=True).then_inc(self_ready, 1)
            for t in range(NT):
                pe.wait_ge(scaled, t + 1)
                if t >= 3:
                    pe.wait_ge(group_copied, t - 2)
                a, b = t * per, min(t * per + per, groups)
                pe.matmul(group_ps[0:GN, t % 3, 0:(b - a) * D], k.relations[:], k.acc[:, a:b, 0:D], start=True,
                          stop=True).then_inc(group_ready, 1)
                pe.matmul(self_ps[:, t // per, (t % per) * D:(t % per + 1) * D], k.x_t[:, t * P:(t + 1) * P], w_self[:],
                          start=True, stop=True).then_inc(self_ready, 1)

        @block.scalar
        def _(act):
            act.wait_ge(cleared, 1)
            for t in range(NT):
                act.wait_ge(group_ready, t + 1)
                w = min(per, groups - t * per)
                nc.scalar.copy(by_group[:, t, 0:w, :], group_ps[0:GN, t % 3, 0:w * D].rearrange("p (j d) -> p j d", d=D)
                               ).then_inc(group_copied, 1)

def layernorm(nc, k, name, x_t=None, out=None):
    with Stage(nc) as c:
        def sb(n, shape, dt=F32):
            return c.enter_context(nc.sbuf_tensor(f"{name}_{n}", shape, dt))

        def sem(n):
            return c.semaphore(f"{name}_{n}")

        mean = sb("mean", [P, NT])
        var = sb("var", [P, NT])
        std = sb("std", [P, NT])
        square = sb("square", [P, NT, D])
        turned = c.enter_context(nc.psum_tensor(f"{name}_turned", [P, 7, CW], F32))
        ln_step, var_ready, std_ready, normed, turned_ready, stored = (sem("step"), sem("var_ready"), sem("std_ready"),
                                                                       sem("normed"), sem("turned_ready"), sem("stored"))
        copied = sem("copied")
        block = c.enter_context(nc.Block())
        halves = ((0, 13), (13, NT))

        @block.vector
        def _(dve):
            step = Steps(dve, ln_step)
            v = nc.vector
            wide = [P, NT, D]
            step(v.tensor_reduce(mean[:], k.pre[:], AX, ALU.add))
            step(v.tensor_scalar(mean[:], mean[:], 1.0 / D, None, ALU.mult))
            step(v.tensor_tensor(k.pre[:], k.pre[:], mean[:].unsqueeze(2).to_broadcast(wide), ALU.subtract))
            step(v.tensor_tensor(square[:], k.pre[:], k.pre[:], ALU.mult))
            v.tensor_reduce(var[:], square[:], AX, ALU.add).then_inc(var_ready, 1)
            dve.wait_ge(std_ready, 1)
            step(v.reciprocal(std[:], std[:]))
            for i, (a, b) in enumerate(halves):
                v.tensor_tensor(k.x_n[:, a:b, :], k.pre[:, a:b, :], std[:, a:b].unsqueeze(2).to_broadcast([P, b - a, D]),
                                ALU.mult).then_inc(normed, 1)
            if x_t is not None:
                for q in range(7):
                    cols = min(CW, NP - q * CW)
                    dve.wait_ge(turned_ready, min(4 * q + 4, NT))
                    if q % 2:
                        v.tensor_copy(x_t[:, q * CW:q * CW + cols], turned[0:D, q, 0:cols]).then_inc(copied, 1)
                dve.wait_ge(copied, 3)

        @block.scalar
        def _(act):
            act.wait_ge(var_ready, 1)
            nc.scalar.activation(std[:], var[:], ACT.Sqrt, bias=k.eps[:, 0:1], scale=1.0 / D).then_inc(std_ready, 1)
            if x_t is not None:
                for q in range(0, 7, 2):
                    cols = min(CW, NP - q * CW)
                    act.wait_ge(turned_ready, min(4 * q + 4, NT))
                    nc.scalar.copy(x_t[:, q * CW:q * CW + cols], turned[0:D, q, 0:cols]).then_inc(std_ready, 1)
                act.wait_ge(std_ready, 5)

        if x_t is not None:
            @block.tensor
            def _(pe):
                for t in range(NT):
                    if t in (0, 13):
                        pe.wait_ge(normed, 1 if t == 0 else 2)
                    pe.transpose(turned[0:D, t // 4, (t % 4) * P:(t % 4 + 1) * P], k.x_n[:, t, :],
                                 k.ident[:]).then_inc(turned_ready, 1)

        if out is not None:
            @block.sync
            def _(sp):
                sp.wait_ge(normed, 2)
                full = N // P
                sp.dma_start(out[0:full * P, :].rearrange("(t p) d -> p t d", p=P), k.x_n[:, 0:full, :]).then_inc(stored, 16)
                sp.dma_start(out[full * P:N, :], k.x_n[0:N - full * P, full, :]).then_inc(stored, 16)
                sp.wait_ge(stored, 32)

def neighbour_sum(nc, k, name, with_degree):
    with Stage(nc) as c:
        def sb(n, shape, dt=F32):
            return c.enter_context(nc.sbuf_tensor(f"{name}_{n}", shape, dt))

        def sem(n):
            return c.semaphore(f"{name}_{n}")

        S = 5
        M = D + 1 if with_degree else D
        rows = sb("rows", [P, S, NP])
        rows_b = sb("rows_b", [P, S, NP], BF16)
        v = sb("v", [P, S, M])
        root = sb("root", [P, S])
        if with_degree:
            heavy = sb("heavy", [P, NT])
            heavy_sum = sb("heavy_sum", [P, 1])
        else:
            rest = sb("rest", [P, NT, D])
            parts = sb("parts", [P, NT, 4, D], BF16)
        total = c.enter_context(nc.psum_tensor(f"{name}_total", [P, DC, CW], F32))
        heavy_ps = c.enter_context(nc.psum_tensor(f"{name}_heavy_ps", [P, CW], F32))
        loaded = [sem(f"loaded{s}") for s in range(S)]
        stored = [sem(f"stored{s}") for s in range(S)]
        v_ready, used, cleared, copied = sem("v_ready"), sem("used"), sem("cleared"), sem("copied")
        deg_step, deg_asked, root_ready = sem("deg_step"), sem("deg_asked"), sem("root_ready")
        short_ready, heavy_ready, heavy_counted, heavy_done = (sem("short_ready"), sem("heavy_ready"),
                                                               sem("heavy_counted"), sem("heavy_done"))
        block = c.enter_context(nc.Block())
        cols = [min(CW, NP - q * CW) for q in range(DC)]

        def either(eng, engine, exact, short):
            if with_degree:
                exact()
                return
            some = nc.values_load_multi_w_load_instructions(
                k.heavy_i[0:1, 0:1], engines=[engine], min_val=0, max_val=NP,
                skip_runtime_bounds_check_because="a number of nodes")[1][0]
            with eng.If(some > 0):
                exact()
            with eng.Else():
                short()

        @block.sync
        def _(sp):
            def stream(to, matrix):
                def body(it, first):
                    for s in range(S):
                        if not first:
                            sp.wait_ge(used, it * S + (s + 1 - S))
                            if with_degree:
                                sp.wait_ge(short_ready, it * S + (s + 1 - S))
                        sp.dma_start(to[:, s, :], matrix[bass.ds(it * (S * P) + s * P, P), :]).then_inc(loaded[s], 16)
                body(0, True)
                with sp.Fori(1, NT // S) as it:
                    body(it, False)

            either(sp, mybir.EngineType.SP, lambda: stream(rows, k.adj_rows), lambda: stream(rows_b, k.adj_short))

        @block.tensor
        def _(pe):
            def clear(m, last):
                for q in range(DC):
                    z = pe.matmul(total[0:m, q, 0:cols[q]], k.zero_b[:, 0:m], k.zero_b[:, 0:cols[q]],
                                  start=not last, stop=last)
                return z

            def exact():
                clear(M, False)
                with pe.Fori(0, NT // S) as it:
                    for s in range(S):
                        pe.wait_ge(loaded[s], it * 16 + 16)
                        pe.wait_ge(v_ready, it * S + (s + 1))
                        for q in range(DC):
                            m = pe.matmul(total[0:M, q, 0:cols[q]], v[:, s, :], rows[:, s, q * CW:q * CW + cols[q]],
                                          start=False, stop=False, skip_group_check=True)
                        m.then_inc(used, 1)
                clear(M, True).then_inc(cleared, 1)

            def short():
                clear(P, False)
                with pe.Fori(0, NT // S) as it:
                    pe.wait_ge(v_ready, it + 1)
                    for s in range(S):
                        pe.wait_ge(loaded[s], it * 16 + 16)
                        for i in (0, 2):
                            two = parts[:, bass.ds(it * S + s, 1), i:i + 2, :].rearrange("p t i d -> p (t i d)")
                            for q in range(DC):
                                m = pe.matmul(total[:, q, 0:cols[q]], two, rows_b[:, s, q * CW:q * CW + cols[q]],
                                              start=False, stop=False, skip_group_check=True)
                        m.then_inc(used, 1)
                clear(P, True).then_inc(cleared, 1)

            either(pe, mybir.EngineType.PE, exact, short)
            if with_degree:
                pe.wait_ge(heavy_ready, 1)
                pe.matmul(heavy_ps[0:1, 0:1], k.ones_f[:, 0:1], heavy_sum[:], start=True, stop=True).then_inc(heavy_counted, 1)

        @block.scalar
        def _(act):
            def take(m):
                act.wait_ge(cleared, 1)
                for q in range(0, DC, 2):
                    nc.scalar.copy(k.agg_t[0:m, q * CW:q * CW + cols[q]], total[0:m, q, 0:cols[q]]).then_inc(copied, 1)
                act.wait_ge(copied, DC)

            def shorten(it, first):
                for s in range(S):
                    act.wait_ge(loaded[s], it * 16 + 16)
                    if not first:
                        act.wait_ge(stored[s], it * 16)
                    nc.scalar.copy(rows_b[:, s, :], rows[:, s, :]).then_inc(short_ready, 1)
                    act.wait_ge(short_ready, it * S + (s + 1))
                    act.dma_start(k.adj_short[bass.ds(it * (S * P) + s * P, P), :], rows_b[:, s, :]).then_inc(stored[s], 16)
                    act.wait_ge(deg_asked, it * S + (s + 1))
                    nc.scalar.activation(root[:, s:s + 1], root[:, s:s + 1], ACT.Sqrt).then_inc(root_ready, 1)

            if with_degree:
                shorten(0, True)
                with act.Fori(1, NT // S) as it:
                    shorten(it, False)
                take(M)
                for s in range(S):
                    act.wait_ge(stored[s], 16 * (NT // S))
            else:
                either(act, mybir.EngineType.Activation, lambda: take(M), lambda: take(P))

        @block.vector
        def _(dve):
            vec = nc.vector
            ch = Chain(dve, deg_step)

            def take(m):
                dve.wait_ge(cleared, 1)
                for q in range(1, DC, 2):
                    vec.tensor_copy(k.agg_t[0:m, q * CW:q * CW + cols[q]], total[0:m, q, 0:cols[q]]).then_inc(copied, 1)

            def body(it, first):
                for s in range(S):
                    tile = bass.ds(it * S + s, 1)
                    if with_degree:
                        dve.wait_ge(loaded[s], it * 16 + 16)
                        ch.step(vec.tensor_reduce(k.out_deg[:, tile], rows[:, s, :], AX, ALU.add))
                        vec.tensor_scalar(root[:, s:s + 1], k.out_deg[:, tile], 1.0, None, ALU.max).then_inc(deg_asked, 1)
                        dve.wait_ge(root_ready, it * S + (s + 1))
                        ch.step(vec.reciprocal(root[:, s:s + 1], root[:, s:s + 1]))
                        feat = k.feat[:, tile, :].rearrange("p t d -> p (t d)")
                        ch.step(vec.tensor_scalar(feat, k.x_n[:, tile, :].rearrange("p t d -> p (t d)"),
                                                  root[:, s:s + 1], None, ALU.mult))
                    else:
                        feat = k.x_n[:, tile, :].rearrange("p t d -> p (t d)")
                    if not first:
                        dve.wait_ge(used, it * S + (s + 1 - S))
                    vec.tensor_scalar(v[:, s, 0:D], feat, 1.0, None, ALU.mult).then_inc(v_ready, 1)

            def exact():
                ch.begin(0)
                if with_degree:
                    ch.step(vec.memset(v[:, :, D:D + 1], 1.0))
                else:
                    ch.step(vec.memset(k.agg_t[D:P, :], 0.0))
                body(0, True)
                start, steps = ch.n, 3 * S if with_degree else 0
                with dve.Fori(1, NT // S) as it:
                    ch.begin((it - 1) * steps + start)
                    body(it, False)
                take(M)

            def short():
                ch.begin(0)
                ch(vec.memset(parts[:, :, 3], 0.0))
                for b in range(NT // S):
                    t = slice(b * S, b * S + S)
                    ch.step(vec.tensor_copy(parts[:, t, 0], k.x_n[:, t]))
                    ch.step(vec.tensor_tensor(rest[:, t], k.x_n[:, t], parts[:, t, 0], ALU.subtract))
                    ch.step(vec.tensor_copy(parts[:, t, 1], rest[:, t]))
                    vec.tensor_tensor(parts[:, t, 2], rest[:, t], parts[:, t, 1], ALU.subtract).then_inc(v_ready, 1)
                take(P)

            either(dve, mybir.EngineType.DVE, exact, short)
            if with_degree:
                vec.tensor_scalar(heavy[:], k.out_deg[:], 256.0, None, ALU.is_gt).then_inc(heavy_done, 1)
                dve.wait_ge(heavy_done, 1)
                vec.tensor_reduce(heavy_sum[:], heavy[:], AX, ALU.add).then_inc(heavy_ready, 1)
                dve.wait_ge(heavy_counted, 1)
                vec.tensor_copy(k.heavy_i[:], heavy_ps[0:1, 0:1]).then_inc(heavy_done, 1)
                dve.wait_ge(heavy_done, 2)

def turn_columns(pe, k, out_ps, src, rows, ready):
    for t in range(NT):
        pe.transpose(out_ps[:, t // 7, (t % 7) * rows:(t % 7 + 1) * rows], src[0:rows, t * P:(t + 1) * P],
                     k.ident[0:rows, 0:rows]).then_inc(ready, 1)

def degree_layer(nc, k):
    with Stage(nc) as c:
        def sb(n, shape, dt=F32):
            return c.enter_context(nc.sbuf_tensor(f"deg_{n}", shape, dt))

        def sem(n):
            return c.semaphore(f"deg_{n}")

        M = D + 1
        w1 = sb("w1", [M, M])
        w2 = sb("w2", [D, M])
        inner = sb("inner", [D, NP])
        rst_t = sb("rst_t", [M, NP])
        root = sb("roots", [P, NT])
        turned = c.enter_context(nc.psum_tensor("deg_turned", [P, 7, CW], F32))
        zeroed, loaded, turned_ready, inner_ready = sem("zeroed"), sem("loaded"), sem("turned"), sem("inner_ready")
        prod_ready, prod_copied, back_ready, root_asked = (sem("prod_ready"), sem("prod_copied"), sem("back_ready"),
                                                           sem("root_asked"))
        step_sem, root_ready = sem("steps"), sem("root_ready")
        block = c.enter_context(nc.Block())
        cols = [min(CW, NP - q * CW) for q in range(DC)]

        @block.gpsimd
        def _(pool):
            nc.gpsimd.memset(w1[:], 0.0).then_inc(zeroed, 1)
            nc.gpsimd.memset(w2[:], 0.0).then_inc(zeroed, 1)
            pool.wait_ge(zeroed, 2)
            nc.gpsimd.memset(w1[D:M, D:M], 1.0).then_inc(zeroed, 1)

        @block.sync
        def _(sp):
            sp.wait_ge(zeroed, 2)
            sp.dma_start(w1[0:D, 0:D], k.w1_1).then_inc(loaded, 16)
            sp.dma_start(w2[:, 0:D], k.w1_2).then_inc(loaded, 16)

        @block.tensor
        def _(pe):
            for t in range(NT):
                pe.transpose(turned[0:D, t // 4, (t % 4) * P:(t % 4 + 1) * P], k.feat[:, t, :],
                             k.ident[:]).then_inc(turned_ready, 1)
            pe.wait_ge(loaded, 32)
            pe.wait_ge(zeroed, 3)
            for q in range(DC):
                pe.wait_ge(inner_ready, q + 1)
                pe.matmul(turned[0:M, q, 0:cols[q]], w1[:], k.agg_t[0:M, q * CW:q * CW + cols[q]], start=True, stop=False)
                pe.matmul(turned[0:M, q, 0:cols[q]], w2[:], inner[:, q * CW:q * CW + cols[q]], start=False,
                          stop=True).then_inc(prod_ready, 1)
            pe.wait_ge(prod_copied, DC)
            turn_columns(pe, k, turned, rst_t, M, back_ready)

        @block.scalar
        def _(act):
            for q in range(DC):
                act.wait_ge(prod_ready, q + 1)
                nc.scalar.copy(rst_t[:, q * CW:q * CW + cols[q]], turned[0:M, q, 0:cols[q]]).then_inc(prod_copied, 1)
            act.wait_ge(root_asked, 4)
            nc.scalar.activation(root[:], root[:], ACT.Sqrt).then_inc(root_ready, 1)

        @block.vector
        def _(dve):
            v = nc.vector
            step = Steps(dve, step_sem)
            for q in range(DC):
                dve.wait_ge(turned_ready, min(4 * q + 4, NT))
                v.tensor_tensor(inner[:, q * CW:q * CW + cols[q]], turned[0:D, q, 0:cols[q]],
                                k.agg_t[0:D, q * CW:q * CW + cols[q]], ALU.mult).then_inc(inner_ready, 1)
            for b in range(4):
                t0, t1 = 7 * b, min(7 * b + 7, NT)
                dve.wait_ge(back_ready, t1)
                part = turned[:, b, 0:(t1 - t0) * M].rearrange("p (t m) -> p t m", m=M)
                v.tensor_scalar(root[:, t0:t1], part[:, :, D], 1.0, None, ALU.max).then_inc(root_asked, 1)
            dve.wait_ge(root_ready, 1)
            step(v.reciprocal(root[:], root[:]))
            for b in range(4):
                t0, t1 = 7 * b, min(7 * b + 7, NT)
                part = turned[:, b, 0:(t1 - t0) * M].rearrange("p (t m) -> p t m", m=M)
                step(v.tensor_tensor(k.pre[:, t0:t1, :], part[:, :, 0:D],
                                     root[:, t0:t1].unsqueeze(2).to_broadcast([P, t1 - t0, D]), ALU.mult))
                step(v.tensor_tensor(k.pre[:, t0:t1, :], k.pre[:, t0:t1, :], k.x_n[:, t0:t1, :], ALU.add))

def linear_layer(nc, k, i):
    last = i == 2
    with Stage(nc) as c:
        def sb(n, shape, dt=F32):
            return c.enter_context(nc.sbuf_tensor(f"lin{i}_{n}", shape, dt))

        def sem(n):
            return c.semaphore(f"lin{i}_{n}")

        w_msg = sb("w_msg", [P, D])
        w_self = sb("w_self", [D, D])
        bias = sb("bias", [D, 1])
        prod = c.enter_context(nc.psum_tensor(f"lin{i}_prod", [P, DC, CW], F32))
        loaded, prod_ready, x_ready, turned_ready, x_copied = (sem("loaded"), sem("prod_ready"), sem("x_ready"),
                                                               sem("turned_ready"), sem("x_copied"))
        block = c.enter_context(nc.Block())
        cols = [min(CW, NP - q * CW) for q in range(DC)]

        @block.sync
        def _(sp):
            sp.dma_start(w_msg[0:D, :], k.w_msg[i]).then_inc(loaded, 16)
            sp.dma_start(w_msg[D:P, :], k.w_msg[i]).then_inc(loaded, 16)
            sp.dma_start(w_self[:], k.w_self2[i]).then_inc(loaded, 16)
            sp.dma_start(bias[:], k.bias2[:, i:i + 1]).then_inc(loaded, 16)

        @block.tensor
        def _(pe):
            pe.wait_ge(loaded, 64)
            for q in range(DC):
                pe.matmul(prod[0:D, q, 0:cols[q]], w_self[:], k.x_t[:, q * CW:q * CW + cols[q]], start=True, stop=False)
                pe.matmul(prod[0:D, q, 0:cols[q]], w_msg[:], k.agg_t[:, q * CW:q * CW + cols[q]], start=False,
                          stop=True).then_inc(prod_ready, 1)
            pe.wait_ge(x_ready, DC)
            turn_columns(pe, k, prod, k.x_t, D, turned_ready)

        @block.scalar
        def _(act):
            for q in range(DC):
                act.wait_ge(prod_ready, q + 1)
                nc.scalar.activation(k.x_t[:, q * CW:q * CW + cols[q]], prod[0:D, q, 0:cols[q]],
                                     ACT.Identity if last else ACT.Relu, bias=bias[:, 0:1]).then_inc(x_ready, 1)

        @block.vector
        def _(dve):
            for b in range(4):
                t0, t1 = 7 * b, min(7 * b + 7, NT)
                dve.wait_ge(turned_ready, t1)
                part = prod[:, b, 0:(t1 - t0) * D].rearrange("p (t m) -> p t m", m=D)
                if last:
                    nc.vector.tensor_tensor(k.pre[:, t0:t1, :], part, k.x_skip[:, t0:t1, :], ALU.add).then_inc(x_copied, 1)
                else:
                    nc.vector.tensor_copy(k.x_n[:, t0:t1, :], part).then_inc(x_copied, 1)

            dve.wait_ge(x_copied, 4)

def keep(nc, k):
    with Stage(nc) as c:
        kept = c.semaphore("kept")
        block = c.enter_context(nc.Block())

        @block.vector
        def _(dve):
            nc.vector.tensor_copy(k.x_skip[:], k.x_n[:]).then_inc(kept, 1)
            dve.wait_ge(kept, 1)

def edge_tables(nc, k):
    with Stage(nc) as c:
        def sb(n, shape, dt=F32):
            return c.enter_context(nc.sbuf_tensor(f"et_{n}", shape, dt))

        def sem(n):
            return c.semaphore(f"et_{n}")

        w1a = sb("w1a", [D, H])
        rest = sb("rest", [P, 2, 4, H])
        b2 = sb("b2", [3, H])
        b2_part = sb("b2_part", [3, 3, H], BF16)
        b2_rest = sb("b2_rest", [3, H])
        b2_sum = sb("b2_sum", [3, H])
        y_ps = c.enter_context(nc.psum_tensor("y_ps", [P, 7, CW], F32))
        loaded, y_ready, step_sem = sem("loaded"), sem("y_ready"), sem("step")
        block = c.enter_context(nc.Block())

        @block.sync
        def _(sp):
            sp.dma_start(w1a[:], k.w1a).then_inc(loaded, 16)
            sp.dma_start(b2[:], k.b2_rows).then_inc(loaded, 16)
            sp.dma_start(k.w1b[:], k.w1b_in).then_inc(loaded, 16)
            sp.dma_start(k.w2[:], k.w2_in).then_inc(loaded, 16)
            sp.dma_start(k.b1[:], k.b1_in).then_inc(loaded, 16)

        @block.tensor
        def _(pe):
            pe.wait_ge(loaded, 80)
            for t in range(NT):
                pe.matmul(y_ps[:, t // 4, (t % 4) * H:(t % 4 + 1) * H], k.x_t[:, t * P:(t + 1) * P], w1a[:],
                          start=True, stop=True).then_inc(y_ready, 1)

        @block.vector
        def _(dve):
            v = nc.vector
            step = Steps(dve, step_sem)
            step(v.memset(k.y[:, NT:NT + 1], 0.0))
            for q in range(7):
                t0, t1 = 4 * q, min(4 * q + 4, NT)
                w = t1 - t0
                dve.wait_ge(y_ready, t1)
                src = y_ps[:, q, 0:w * H].rearrange("p (t h) -> p t h", h=H)
                step(v.tensor_copy(k.y[:, t0:t1, 0], src))
                step(v.tensor_tensor(rest[:, q % 2, 0:w], src, k.y[:, t0:t1, 0], ALU.subtract))
                step(v.tensor_copy(k.y[:, t0:t1, 1], rest[:, q % 2, 0:w]))
                step(v.tensor_tensor(k.y[:, t0:t1, 2], rest[:, q % 2, 0:w], k.y[:, t0:t1, 1], ALU.subtract))
            dve.wait_ge(loaded, 80)
            step(v.tensor_copy(b2_part[:, 0], b2[:]))
            step(v.tensor_tensor(b2_rest[:], b2[:], b2_part[:, 0], ALU.subtract))
            step(v.tensor_copy(b2_part[:, 1], b2_rest[:]))
            step(v.tensor_tensor(b2_part[:, 2], b2_rest[:], b2_part[:, 1], ALU.subtract))
            step(v.tensor_scalar(b2_sum[:], b2_part[:, 0], k.ident[0:3, 0:1], None, ALU.mult))
            for i in (1, 2):
                step(v.scalar_tensor_tensor(b2_sum[:], b2_part[:, i], k.ident[0:3, i:i + 1], b2_sum[:], ALU.mult, ALU.add))
            step(v.tensor_copy(k.b2_parts[:], b2_sum[:]))
            step(v.memset(k.ones_b[:], 1.0))

def edge_loop(nc, k):
    with Stage(nc) as c:
        def sb(n, shape, dt=F32):
            return c.enter_context(nc.sbuf_tensor(f"el_{n}", shape, dt))

        def ps(n, shape, dt=F32):
            return c.enter_context(nc.psum_tensor(f"el_{n}", shape, dt))

        def sem(n):
            return c.semaphore(f"el_{n}")

        rec = sb("rec", [P, 2, B, RW])
        ends = sb("ends", [P, 2, B, 2])
        near = sb("near", [P, 2, B])
        miss = sb("miss", [P, 2, B, P], BF16)
        hit_t = sb("hit_t", [P, 2, B, P], BF16)
        low = sb("low", [P, 2, B])
        valid = sb("valid", [P, 2, B])
        join = sb("join", [P, 2, B, P])
        rank = sb("rank", [P, 2, B])
        later = sb("later", [P, 2, B])
        place = sb("place", [P, 2, B])
        idx = sb("idx", [P, 4, 4], U32)
        ea_t = sb("ea_t", [D, 2, CW])
        h1 = sb("h1", [P, 2, CW])
        h2 = sb("h2", [P, 2, 4, H])
        rows = sb("rows", [P, 4, 4, H])
        miss_t = ps("miss_t", [P, B, P], BF16)
        src_t = ps("src_t", [P, B, P])
        ea_ps = ps("ea_ps", [P, CW])
        h1_ps = ps("h1_ps", [P, CW])
        h2_ps = ps("h2_ps", [P, CW])
        sum_ps = ps("sum_ps", [P, 2, CW])
        rec_loaded = [sem(f"rec_loaded{s}") for s in range(2)]
        added = [sem(f"added{a}") for a in range(NACC)]
        step_sem, ends_ready, miss_ready, miss_t_ready, hit_t_ready = (sem("step"), sem("ends_ready"), sem("miss_ready"),
                                                                       sem("miss_t_ready"), sem("hit_t_ready"))
        src_t_ready, join_ready, ea_ready, ea_copied = (sem("src_t_ready"), sem("join_ready"), sem("ea_ready"),
                                                        sem("ea_copied"))
        h1_ready, h1_done, h2_ready, h2_done, sum_ready, rows_ready, passed = (
            sem("h1_ready"), sem("h1_done"), sem("h2_ready"), sem("h2_done"), sem("sum_ready"), sem("rows_ready"),
            sem("passed"))
        block = c.enter_context(nc.Block())
        IT = NB3 // 2
        Q = 2 * NB3

        @block.sync
        def _(sp):
            def body(it, first):
                for s in range(2):
                    _, offs = nc.values_load_multi_w_load_instructions(
                        k.visit_row[0:1, 2, bass.ds(it * (2 * B) + s * B, B)], engines=[mybir.EngineType.SP],
                        min_val=0, max_val=EP, skip_runtime_bounds_check_because="clamped to the table's end")
                    if not first:
                        sp.wait_ge(ends_ready, it * 2 + (s - 1))
                        sp.wait_ge(ea_ready, it * 4 + (2 * s - 2))
                    for u in range(B):
                        sp.dma_start(rec[:, s, u, :], k.rec[bass.ds(offs[u], P), :]).then_inc(rec_loaded[s], 16)
            body(0, True)
            with sp.Fori(1, IT) as it:
                body(it, False)

        @block.gpsimd
        def _(pool):
            def body(it, first):
                for j in range(4):
                    pool.wait_ge(rows_ready, it * 4 + (j + 1))
                    pool.sem_inc(passed, 1)
                    for a in range(NACC):
                        if not (first and j == 0):
                            pool.wait_ge(added[a], it * 64 + 16 * j)
                            pool.sem_inc(passed, 1)
                        pool.indirect_dma_start(k.sums_flat[a], bass.IndirectOffsetOnAxis(idx[:, j, a:a + 1], 0),
                                                rows[:, j, a, :], None, compute_op=ALU.add).then_inc(added[a], 16)
            body(0, True)
            with pool.Fori(1, IT) as it:
                body(it, False)
            for a in range(NACC):
                pool.wait_ge(added[a], 16 * Q)

        @block.tensor
        def _(pe):
            def turn_ends(m, s, first):
                pe.wait_ge(miss_ready, m + 1)
                if not first:
                    pe.wait_ge(hit_t_ready, m)
                for u in range(B):
                    t = pe.transpose(miss_t[:, u, :], miss[:, s, u, :], k.ident_b[:])
                t.then_inc(miss_t_ready, 1)
                pe.wait_ge(ends_ready, m + 1)
                if not first:
                    pe.wait_ge(join_ready, m)
                for u in range(B):
                    t = pe.transpose(src_t[:, u, :], ends[:, s, u, 0:1].to_broadcast([P, P]), k.ident[:])
                t.then_inc(src_t_ready, 1)

            def turn_features(q, j, loads, first):
                s, h = (j // 2) % 2, j % 2
                if h == 0:
                    pe.wait_ge(rec_loaded[s], loads)
                if not first:
                    pe.wait_ge(ea_copied, q)
                pe.sem_inc(passed, 1)
                for u in range(4):
                    t = pe.transpose(ea_ps[0:D, u * P:(u + 1) * P], rec[:, s, 4 * h + u, 4:RW], k.ident[:])
                t.then_inc(ea_ready, 1)

            def tiles_of(m):
                return nc.values_load_multi_w_load_instructions(
                    k.visit_row[0:1, 3, bass.ds(m * B, B)], engines=[mybir.EngineType.PE],
                    min_val=0, max_val=NT, skip_runtime_bounds_check_because="clamped to the spare tile")[1]

            def product1(q, j, n1, tiles, first):
                s, h = (j // 2) % 2, j % 2
                pe.wait_ge(ea_copied, q + 1)
                pe.wait_ge(hit_t_ready, n1)
                if not first:
                    pe.wait_ge(h1_done, q)
                for u in range(4):
                    pe.matmul(h1_ps[:, u * P:(u + 1) * P], k.w1b[:], ea_t[:, j % 2, u * P:(u + 1) * P], start=True,
                              stop=False)
                    for i in range(3):
                        m = pe.matmul(h1_ps[:, u * P:(u + 1) * P],
                                      k.y[:, bass.ds(tiles[4 * h + u], 1), i, :].rearrange("p t h -> p (t h)"),
                                      hit_t[:, s, 4 * h + u, :], start=False, stop=(i == 2))
                m.then_inc(h1_ready, 1)

            def product2(q, j, first):
                pe.wait_ge(h1_done, q + 1)
                if not first:
                    pe.wait_ge(h2_done, q)
                for u in range(4):
                    pe.matmul(h2_ps[:, u * P:(u + 1) * P], k.ones_b[:], k.b2_parts[:], start=True, stop=False)
                    m = pe.matmul(h2_ps[:, u * P:(u + 1) * P], h1[:, j % 2, u * P:(u + 1) * P], k.w2[:], start=False,
                                  stop=True)
                m.then_inc(h2_ready, 1)

            def join_rows(q, j, n1, first):
                s, h = (j // 2) % 2, j % 2
                pe.wait_ge(h2_done, q + 1)
                pe.wait_ge(join_ready, n1)
                if not first:
                    pe.wait_ge(rows_ready, q - 1)
                for u in range(4):
                    m = pe.matmul(sum_ps[:, j % 2, u * P:(u + 1) * P], join[:, s, 4 * h + u, :], h2[:, j % 2, u, :],
                                  start=True, stop=True)
                m.then_inc(sum_ready, 1)

            state = {}

            def body(it, first, last):
                for j in range(4):
                    q = it * 4 + j
                    s, h = j // 2, j % 2
                    if h == 0 and not (last and s == 1):
                        turn_ends(it * 2 + (s + 1), 1 - s, False)
                    if not (last and j >= 2):
                        turn_features(q + 2, (j + 2) % 4, it * (16 * B) + 16 * B * (1 if s == 0 else 2), False)
                    if h == 0 and not (first and j == 0):
                        join_rows(q - 1, (j - 1) % 4, it * 2 + (s + h), first and j < 3)
                    if not (last and j == 3):
                        if h == 1:
                            tiles = state["next"] = tiles_of(it * 2 + (s + 1))
                        else:
                            tiles = state["now"] if s == 0 else state["next"]
                        product1(q + 1, (j + 1) % 4, it * 2 + (s + 1 + h), tiles, False)
                    if h == 1:
                        join_rows(q - 1, (j - 1) % 4, it * 2 + (s + h), first and j < 3)
                    product2(q, j, first and j == 0)

            def lead(it):
                state["now"] = tiles_of(it * 2)

            turn_ends(0, 0, True)
            turn_features(0, 0, 16 * B, True)
            turn_features(1, 1, 16 * B, False)
            lead(0)
            product1(0, 0, 1, state["now"], True)
            body(0, True, False)
            with pe.Fori(1, IT - 1) as it:
                lead(it)
                body(it, False, False)
            lead(IT - 1)
            body(IT - 1, False, True)
            join_rows(Q - 1, 3, NB3, False)

        @block.scalar
        def _(act):
            a = nc.scalar

            def masks(m, s, first):
                act.wait_ge(miss_t_ready, m + 1)
                if not first:
                    act.wait_ge(h1_ready, m * 2 - 2)
                a.activation(hit_t[:, s], miss_t[:], ACT.Identity, bias=k.ones_f[:, 0:1], scale=-1.0).then_inc(hit_t_ready, 1)

            def features(q, j, first):
                act.wait_ge(ea_ready, q + 1)
                if not first:
                    act.wait_ge(h1_ready, q - 1)
                a.copy(ea_t[:, j % 2, :], ea_ps[0:D, :]).then_inc(ea_copied, 1)

            def relu1(q, j, first):
                act.wait_ge(h1_ready, q + 1)
                if not first:
                    act.wait_ge(h2_ready, q - 1)
                a.activation(h1[:, j % 2, :], h1_ps[:], ACT.Relu, bias=k.b1[:, 0:1]).then_inc(h1_done, 1)

            def relu2(q, j, n1, first):
                s, h = (j // 2) % 2, j % 2
                act.wait_ge(h2_ready, q + 1)
                act.wait_ge(join_ready, n1)
                if not first:
                    act.wait_ge(sum_ready, q - 1)
                for u in range(4):
                    m = a.activation(h2[:, j % 2, u, :], h2_ps[:, u * P:(u + 1) * P], ACT.Relu,
                                     scale=valid[:, s, 4 * h + u:4 * h + u + 1])
                m.then_inc(h2_done, 1)

            def body(it, first, last):
                for j in range(4):
                    q = it * 4 + j
                    s, h = j // 2, j % 2
                    if h == 0 and not (last and s == 1):
                        masks(it * 2 + (s + 1), 1 - s, first and s == 0)
                    if not (last and j >= 2):
                        features(q + 2, (j + 2) % 4, False)
                    if not (last and j == 3):
                        relu1(q + 1, (j + 1) % 4, first and j == 0)
                    relu2(q, j, it * 2 + (s + 1), first and j < 2)

            masks(0, 0, True)
            features(0, 0, True)
            features(1, 1, True)
            relu1(0, 0, True)
            body(0, True, False)
            with act.Fori(1, IT - 1) as it:
                body(it, False, False)
            body(IT - 1, False, True)

        @block.vector
        def _(dve):
            v = nc.vector
            ch = Chain(dve, step_sem)

            def ends_of(m, s, loads, first):
                dve.wait_ge(rec_loaded[s], loads)
                v.tensor_copy(ends[:, s], rec[:, s, :, 2:4]).then_inc(ends_ready, 1)
                dve.wait_ge(ends_ready, m + 1)
                ch.step(v.tensor_tensor(near[:, s], ends[:, s, :, 1], k.tile_base[:, bass.ds(m * B, B)], ALU.subtract))
                if not first:
                    dve.wait_ge(miss_t_ready, m - 1)
                v.tensor_tensor(miss[:, s], near[:, s].unsqueeze(2).to_broadcast([P, B, P]),
                                k.iota_row[:].unsqueeze(1).to_broadcast([P, B, P]), ALU.not_equal).then_inc(miss_ready, 1)

            def joins_of(m, s, first):
                dve.wait_ge(src_t_ready, m + 1)
                if not first:
                    dve.wait_ge(sum_ready, m * 2 - 2)
                for u in range(B):
                    ch(v.scalar_tensor_tensor(join[:, s, u], src_t[:, u, :], ends[:, s, u, 0:1], k.tri[:],
                                              ALU.is_equal, ALU.mult, accum_out=rank[:, s, u:u + 1]))
                ch(v.tensor_scalar(low[:, s], near[:, s], 0.0, None, ALU.is_ge))
                ch.step(v.tensor_scalar(place[:, s], ends[:, s, :, 0], k.spare_col[:, 0:1], -1.0, ALU.subtract, ALU.mult))
                ch(v.tensor_scalar(later[:, s], rank[:, s], 1.5, None, ALU.is_ge))
                ch.step(v.scalar_tensor_tensor(valid[:, s], near[:, s], float(P), low[:, s], ALU.is_lt, ALU.mult))
                ch.step(v.tensor_tensor(place[:, s], place[:, s], later[:, s], ALU.mult))
                v.tensor_tensor(place[:, s], place[:, s], ends[:, s, :, 0], ALU.add).then_inc(join_ready, 1)

            def hand_over(q, j, done, n1):
                s, h = (j // 2) % 2, j % 2
                dve.wait_ge(sum_ready, q + 1)
                dve.wait_ge(join_ready, n1)
                if done is not None:
                    for a in range(NACC):
                        dve.wait_ge(added[a], done)
                ch(v.tensor_copy(idx[:, j], place[:, s, 4 * h:4 * h + 4]))
                ch.wait()
                v.tensor_copy(rows[:, j].rearrange("p u h -> p (u h)"), sum_ps[:, j % 2, :]).then_inc(rows_ready, 1)

            def body(it, first, last):
                for j in range(4):
                    q = it * 4 + j
                    s, h = j // 2, j % 2
                    if h == 1 and not last:
                        ends_of(it * 2 + (s + 2), s, it * (16 * B) + 32 * B, False)
                    if not (first and j == 0):
                        hand_over(q - 1, (j - 1) % 4, None if first and j <= 4 else it * 64 + 16 * (j - 4),
                                  it * 2 + (s + h))
                    if h == 0 and not (last and s == 1):
                        joins_of(it * 2 + (s + 1), 1 - s, first and s == 0)

            ch.begin(0)
            for s in range(2):
                ends_of(s, s, 16 * B, True)
            joins_of(0, 0, True)
            body(0, True, False)
            start = ch.n
            steps = 4 * 1 + 2 * (B + 5) + 2
            with dve.Fori(1, IT - 1) as it:
                ch.begin((it - 1) * steps + start)
                body(it, False, False)
                assert ch.n == steps, ch.n
            ch.begin((IT - 2) * steps + start)
            body(IT - 1, False, True)
            hand_over(Q - 1, 3, 16 * (Q - 4), NB3)

def node_update(nc, k):
    with Stage(nc) as c:
        def sb(n, shape, dt=F32):
            return c.enter_context(nc.sbuf_tensor(f"nu_{n}", shape, dt))

        def sem(n):
            return c.semaphore(f"nu_{n}")

        part = sb("part", [P, NACC, NT, H])
        share = sb("share", [P, NT])
        mean_t = sb("mean_t", [H, NP])
        z = sb("z", [H, NP])
        o_t = sb("o_t", [D, NP])
        wa_x, wa_m, wa_u = sb("wa_x", [D, H]), sb("wa_m", [H, H]), sb("wa_u", [DU, H])
        wb, ba, bb, u0, ba_u = sb("wb", [H, D]), sb("ba", [H, 1]), sb("bb", [D, 1]), sb("u0", [DU, 1]), sb("ba_u", [H, 1])
        ps = c.enter_context(nc.psum_tensor("nu_ps", [P, 7, CW], F32))
        ps_u = c.enter_context(nc.psum_tensor("nu_ps_u", [P, CW], F32))
        loaded, w_loaded, step_sem, mean_ready, turned, u_ready, ba_ready = (
            sem("loaded"), sem("w_loaded"), sem("step"), sem("mean_ready"), sem("turned"), sem("u_ready"), sem("ba_ready"))
        mean_copied, z_ready, z_done, o_ready, o_done, back, pre_done = (
            sem("mean_copied"), sem("z_ready"), sem("z_done"), sem("o_ready"), sem("o_done"), sem("back"), sem("pre_done"))
        block = c.enter_context(nc.Block())
        cols = [min(CW, NP - q * CW) for q in range(DC)]

        @block.sync
        def _(sp):
            for a in range(NACC):
                sp.dma_start(part[:, a], k.sums_flat[a][0:NP, :].rearrange("(t p) h -> p t h", p=P)).then_inc(loaded, 16)
            for dst, src in ((wa_x, k.wa_x), (wa_m, k.wa_m), (wa_u, k.wa_u), (wb, k.wb), (ba, k.ba), (bb, k.bb), (u0, k.u0)):
                sp.dma_start(dst[:], src).then_inc(w_loaded, 16)

        @block.tensor
        def _(pe):
            pe.wait_ge(w_loaded, 112)
            pe.matmul(ps_u[:, 0:1], wa_u[:], u0[:], start=True, stop=True).then_inc(u_ready, 1)
            for t in range(NT):
                if t == 0:
                    pe.wait_ge(mean_ready, 1)
                pe.transpose(ps[:, t // 4, (t % 4) * P:(t % 4 + 1) * P], part[:, 0, t, :], k.ident[:]).then_inc(turned, 1)
            for q in range(DC):
                pe.wait_ge(mean_copied, q + 1)
                pe.matmul(ps[:, q, 0:cols[q]], wa_x[:], k.x_t[:, q * CW:q * CW + cols[q]], start=True, stop=False)
                pe.matmul(ps[:, q, 0:cols[q]], wa_m[:], mean_t[:, q * CW:q * CW + cols[q]], start=False,
                          stop=True).then_inc(z_ready, 1)
            for q in range(DC):
                pe.wait_ge(z_done, q + 1)
                pe.matmul(ps[0:D, q, 0:cols[q]], wb[:], z[:, q * CW:q * CW + cols[q]], start=True,
                          stop=True).then_inc(o_ready, 1)
            pe.wait_ge(o_done, DC)
            turn_columns(pe, k, ps, o_t, D, back)

        @block.scalar
        def _(act):
            act.wait_ge(ba_ready, 1)
            for q in range(DC):
                act.wait_ge(z_ready, q + 1)
                nc.scalar.activation(z[:, q * CW:q * CW + cols[q]], ps[:, q, 0:cols[q]], ACT.Relu,
                                     bias=ba_u[:, 0:1]).then_inc(z_done, 1)
            for q in range(DC):
                act.wait_ge(o_ready, q + 1)
                nc.scalar.activation(o_t[:, q * CW:q * CW + cols[q]], ps[0:D, q, 0:cols[q]], ACT.Identity,
                                     bias=bb[:, 0:1]).then_inc(o_done, 1)

        @block.vector
        def _(dve):
            v = nc.vector
            step = Steps(dve, step_sem)
            dve.wait_ge(u_ready, 1)
            v.tensor_tensor(ba_u[:], ps_u[:, 0:1], ba[:], ALU.add).then_inc(ba_ready, 1)
            step(v.tensor_scalar(share[:], k.out_deg[:], 1.0, None, ALU.max))
            step(v.reciprocal(share[:], share[:]))
            dve.wait_ge(loaded, 16 * NACC)
            for a in range(1, NACC):
                step(v.tensor_tensor(part[:, 0], part[:, 0], part[:, a], ALU.add))
            v.tensor_tensor(part[:, 0], part[:, 0], share[:].unsqueeze(2).to_broadcast([P, NT, H]),
                            ALU.mult).then_inc(mean_ready, 1)
            for q in range(DC):
                dve.wait_ge(turned, min(4 * q + 4, NT))
                v.tensor_copy(mean_t[:, q * CW:q * CW + cols[q]], ps[:, q, 0:cols[q]]).then_inc(mean_copied, 1)
            for b in range(4):
                t0, t1 = 7 * b, min(7 * b + 7, NT)
                dve.wait_ge(back, t1)
                v.tensor_tensor(k.pre[:, t0:t1, :], k.x_n[:, t0:t1, :],
                                ps[:, b, 0:(t1 - t0) * D].rearrange("p (t m) -> p t m", m=D), ALU.add).then_inc(pre_done, 1)
            dve.wait_ge(pre_done, 4)

class Shared:
    pass

def gnn_stack_kernel(nc, x_rows, x_cols, src, dst, edge_type, edge_attr, w_cat, w_t, att_src, att_dst,
                     w_self0, bias0, w1_1, w1_2, w_msg, w_self2, bias2,
                     w1a, w1b, w2, b1, b2_rows, wa_x, wa_m, wa_u, u0, wb, ba, bb, out):
    k = Shared()
    k.x_rows, k.x_cols, k.src, k.dst, k.type, k.edge_attr = x_rows, x_cols, src, dst, edge_type, edge_attr
    k.w_cat, k.w_t, k.att_src, k.att_dst = w_cat, w_t, att_src, att_dst

    k.w_self0, k.bias0, k.w1_1, k.w1_2 = w_self0, bias0, w1_1, w1_2
    k.w_msg, k.w_self2, k.bias2 = w_msg, w_self2, bias2

    k.w1a, k.w1b_in, k.w2_in, k.b1_in, k.b2_rows = w1a, w1b, w2, b1, b2_rows
    k.wa_x, k.wa_m, k.wa_u, k.u0, k.wb, k.ba, k.bb = wa_x, wa_m, wa_u, u0, wb, ba, bb

    def dram(name, shape, dt=F32):
        return nc.dram_tensor(name, shape, dt, kind="Internal").ap()

    adj = dram("adj", [TRASH + 8 * P, 1])
    k.adj = adj
    k.adj_rows = adj[0:TRASH, :].rearrange("(s d) o -> s (d o)", d=NP)
    k.adj_spare = adj[TRASH:TRASH + 8 * P, :].rearrange("(p a) o -> p (a o)", a=8)
    k.sums_flat = [dram(f"sums{a}", [NP + P, H]) for a in range(NACC)]
    k.meta = dram("meta", [EP + P, 4])
    k.meta_copy = dram("meta_copy", [EP, 4])
    k.rec = dram("records", [2 * (EP + P), RW])
    k.adj_short = dram("adj_short", [NP, NP], BF16)
    k.zero_dmas = ZERO_NEXT + 2 * (NT - ZERO_NEXT) + 1
    k.count_row = dram("count_row", [GW])
    k.visit_i = dram("visit_i", [4, NV], I32)
    k.visit_f = dram("visit_f", [2, NV + 1])
    k.table = dram("table", [NP * R, TW])
    k.score_row = dram("score_row", [2, NP * R])
    with ExitStack() as c:
        def sb(name, shape, dt=F32):
            return c.enter_context(nc.sbuf_tensor(name, shape, dt))

        c.enter_context(nc.allow_non_contiguous_dma(reason="tables of a few thousand words, laid out once"))
        k.iota_row = sb("iota_row", [P, P])
        k.iota_p = sb("iota_p", [P, 1])
        k.visit_col = sb("visit_col", [P, B])
        k.trash_col = sb("trash_col", [P, 8])
        k.spare_col = sb("spare_col", [P, 1])
        k.ones_f = sb("ones_f", [P, P])
        k.ident = sb("ident", [P, P])
        k.ident_b = sb("ident_b", [P, P], BF16)
        k.big_ident = sb("big_ident", [P, P], BF16)
        k.zero_b = sb("zero_b", [P, CW], BF16)
        k.tri = sb("tri", [P, P])
        k.below = sb("below", [P, P])
        k.count_w = sb("count_w", [P, 7 * P])
        k.relations = sb("relations", [P, GN])
        k.block_mask = sb("block_mask", [P, 8])
        k.minus_one = sb("minus_one", [P, 1])
        k.unsorted_i = sb("unsorted_i", [1, 1], I32)
        k.aside_i = sb("aside_i", [1, 1], I32)
        k.zero_f = sb("zero_f", [P, 16])
        k.out_deg = sb("out_deg", [P, NT])
        k.adj_key = sb("adj_key", [P, AE])
        k.x_n = sb("x_n", [P, NT, D])
        k.pre = sb("pre", [P, NT, D])
        k.eps = sb("eps", [P, 1])
        k.x_t = sb("x_t", [D, NP])
        k.visit_row = sb("visit_row", [1, 4, NV], I32)
        k.tile_base = sb("tile_base", [P, NV])
        k.zero_written = c.enter_context(nc.semaphore("zero_written"))
        with ExitStack() as c0:
            def sb0(name, shape, dt=F32):
                return c0.enter_context(nc.sbuf_tensor(name, shape, dt))
            k.zero = sb0("zero", [P, NP + P])
            k.group_f = sb0("group_f", [P, EC])
            k.starts = sb0("starts", [P, GW])
            constants(nc, k)
            edge_keys(nc, k)
            schedule(nc, k)
            group_records(nc, k)
            with ExitStack() as c1:
                def sb1(name, shape, dt=F32):
                    return c1.enter_context(nc.sbuf_tensor(name, shape, dt))
                k.self_v = sb1("self_v", [P, NV])
                k.dst_v = sb1("dst_v", [P, NV])
                k.fresh = sb1("fresh", [P, NV])
                k.key_base = sb1("key_base", [P, NV])
                k.tile_f = sb1("tile_f", [P, NV])
                k.acc = sb1("acc", [P, NG + 1, TW])
                node_tables(nc, k)
                attention(nc, k)
                finish_attention(nc, k)
        layernorm(nc, k, "ln0", x_t=k.x_t)
        with ExitStack() as c2:
            def sb2(name, shape, dt=F32):
                return c2.enter_context(nc.sbuf_tensor(name, shape, dt))
            k.agg_t = sb2("agg_t", [P, NP])
            k.heavy_i = sb2("heavy_i", [1, 1], I32)
            k.feat = sb2("feat", [P, NT, D])
            k.x_skip = sb2("x_skip", [P, NT, D])
            neighbour_sum(nc, k, "sum1", True)
            degree_layer(nc, k)
            layernorm(nc, k, "ln1", x_t=k.x_t)
            keep(nc, k)
            for i in range(3):
                neighbour_sum(nc, k, f"sum2{i}", False)
                linear_layer(nc, k, i)
            layernorm(nc, k, "ln2", x_t=k.x_t)
        with ExitStack() as c3:
            def sb3(name, shape, dt=F32):
                return c3.enter_context(nc.sbuf_tensor(name, shape, dt))
            k.y = sb3("y", [P, NT + 1, 3, H], BF16)
            k.w1b = sb3("w1b", [D, H])
            k.w2 = sb3("w2", [H, H])
            k.b1 = sb3("b1", [H, 1])
            k.b2_parts = sb3("b2_parts", [3, H], BF16)
            k.ones_b = sb3("ones_b", [3, P], BF16)
            edge_tables(nc, k)
            edge_loop(nc, k)
        node_update(nc, k)
        layernorm(nc, k, "ln3", out=out)

def layout(i):
    import numpy as np

    def pad(a, rows, value):
        return np.concatenate([a, np.full((rows - a.shape[0],) + a.shape[1:], value, a.dtype)])

    w, w1, wa = i["L0_gnn_W"], i["L3_gnn_W1"], i["L3_gnn_Wa"]
    x = pad(i["x"], NP, 0)
    arrays = {
        "x_rows": x, "x_cols": x.T,
        "src": pad(i["src"], EP + P, PAD_NODE), "dst": pad(i["dst"], EP + P, PAD_NODE),
        "edge_type": pad(i["edge_type_8"], EP + P, 0), "edge_attr": pad(i["edge_attr_64"], EP + P, 0),
        "w_cat": w.transpose(1, 0, 2).reshape(D, R * D), "w_t": w.transpose(2, 0, 1).reshape(D, R * D),
        "att_src": i["L0_gnn_att_src"].T, "att_dst": i["L0_gnn_att_dst"].T,
        "w_self0": i["L0_gnn_W_self"], "bias0": np.concatenate([i["L0_gnn_b_self"][None], i["L0_gnn_bias"]]),
        "w1_1": i["L1_gnn_weight1"], "w1_2": i["L1_gnn_weight2"],
        "w_msg": i["L2_gnn_W_msg"], "w_self2": i["L2_gnn_W_self"], "bias2": i["L2_gnn_b"].T,
        "w1a": w1[:, :D].T, "w1b": w1[:, D:].T, "w2": i["L3_gnn_W2"].T, "b1": i["L3_gnn_b1"][:, None],
        "b2_rows": np.tile(i["L3_gnn_b2"][None], (3, 1)),
        "wa_x": wa[:, :D].T, "wa_m": wa[:, D:D + H].T, "wa_u": wa[:, D + H:].T, "u0": i["L3_gnn_u"][0][:, None],
        "wb": i["L3_gnn_Wb"].T, "ba": i["L3_gnn_ba"][:, None], "bb": i["L3_gnn_bb"][:, None],
    }
    return {name: np.ascontiguousarray(a) for name, a in arrays.items()}

def kernel(**inputs):
    import numpy as np
    import concourse.bacc as bacc
    from concourse.bass_utils import run_bass_kernel_spmd

    nc = bacc.Bacc("TRN2", target_bir_lowering=False, num_devices=1)
    arrays, args = {}, []
    for name, a in layout({name: np.asarray(a) for name, a in inputs.items()}).items():
        arrays[f"in_{name}"] = a
        args.append(nc.dram_tensor(f"in_{name}", a.shape, mybir.dt.from_np(a.dtype), kind="ExternalInput").ap())
    args.append(nc.dram_tensor("out", (N, D), F32, kind="ExternalOutput").ap())
    gnn_stack_kernel(nc, *args)
    return run_bass_kernel_spmd(nc, [arrays], core_ids=[0]).results[0]["out"]
```
